# Optimizing a Trainium2 kernel written in Bass

```python
import numpy as np
import jax
import jax.numpy as jnp

def _softmax(x, axis=-1):
    return jax.nn.softmax(x, axis=axis)

def _gelu(x):
    return jax.nn.gelu(x, approximate=True)

def _silu(x):
    return jax.nn.silu(x)

def _sigmoid(x):
    return jax.nn.sigmoid(x)

def _layernorm(x, axis=-1, eps=1e-05):
    m = jnp.mean(x, axis=axis, keepdims=True)
    v = jnp.var(x, axis=axis, keepdims=True)
    return (x - m) / jnp.sqrt(v + eps)

def _scatter_add(tgt, idx, src, axis=0):
    return tgt.at[idx].add(src)

def _segment_sum(src, seg, n):
    return jax.ops.segment_sum(src, seg, n)
kernel_name = 'mk_xattn_seq_d2_seqx_r4_aa091e'

def setup_inputs(seed: int=0):
    np.random.seed(seed)
    _w = jnp.asarray

    def _rec_inputs():
        import jax
        import jax.numpy as jnp
        _rk = jax.random.key(seed)
        x = -0.0005207 + 1.001 * jax.random.normal(jax.random.fold_in(_rk, 1), (16, 256, 256), jnp.float32)
        _lenS = 256 - jax.random.randint(jax.random.fold_in(_rk, 7), (16,), 0, max(1, 256 // 4) + 1, jnp.int32)
        _lenS2 = 256 - jax.random.randint(jax.random.fold_in(_rk, 8), (16,), 0, max(1, 256 // 4) + 1, jnp.int32)
        _ctx_1024P = jax.random.normal(jax.random.fold_in(_rk, 11), (16, 16, 256), jnp.float32)
        _ctx_1024c = jax.random.dirichlet(jax.random.fold_in(_rk, 511), 0.3 * jnp.ones((16,), jnp.float32), (16, 256))
        _ctx_1024t = jnp.einsum('bsk,bkd->bsd', _ctx_1024c, _ctx_1024P)
        _ctx_1024t = _ctx_1024t * jax.lax.rsqrt(jnp.mean(jnp.square(_ctx_1024t)) + 1e-12) * 0.953939
        ctx_1024 = -0.000514642 + 1.00011 * (_ctx_1024t + 0.3 * jax.random.normal(jax.random.fold_in(_rk, 611), (16, 256, 256), jnp.float32))
        fside_Bx16xSxS2_0 = -1.47943e-05 + 1.00017 * jax.random.normal(jax.random.fold_in(_rk, 12), (16, 16, 256, 256), jnp.float32)
        return (x, ctx_1024, fside_Bx16xSxS2_0)
    x, ctx_1024, fside_Bx16xSxS2_0 = _rec_inputs()

    def _L0_xattn_setup():
        import jax, jax.numpy as jnp
        import numpy as np
        N_HEADS = 16
        D_MODEL = 256
        D_K = 64
        D_V = 64
        LN_EPS = 1e-06
        key = jax.random.key(seed)
        ks = jax.random.split(key, 16)
        B, L, D = (4, 128, D_MODEL)
        s = 1.0 / np.sqrt(D)
        return {'q': jax.random.normal(ks[0], (B, L, D), jnp.float32), 'k': jax.random.normal(ks[1], (B, L, D), jnp.float32), 'v': jax.random.normal(ks[2], (B, L, D), jnp.float32), 'bias': jax.random.normal(ks[3], (B, N_HEADS, L, L), jnp.float32), 'graph_attn_bias': jax.random.normal(ks[4], (B, N_HEADS, L, L), jnp.float32), 'wq': jax.random.normal(ks[5], (D, N_HEADS * D_K), jnp.float32) * s, 'bq': jnp.zeros((N_HEADS * D_K,), jnp.float32), 'wk': jax.random.normal(ks[6], (D, N_HEADS * D_K), jnp.float32) * s, 'bk': jnp.zeros((N_HEADS * D_K,), jnp.float32), 'wv': jax.random.normal(ks[7], (D, N_HEADS * D_V), jnp.float32) * s, 'bv': jnp.zeros((N_HEADS * D_V,), jnp.float32), 'wo': jax.random.normal(ks[8], (N_HEADS * D_V, D), jnp.float32) * s, 'bo': jnp.zeros((D,), jnp.float32), 'ln_g': jnp.ones((D,), jnp.float32), 'ln_b': jnp.zeros((D,), jnp.float32)}
    _L0_xattn_all = _L0_xattn_setup()
    _L0_xattn_in = {k: v for k, v in _L0_xattn_all.items() if k in ('wq', 'bq', 'wk', 'bk', 'wv', 'bv', 'wo', 'bo', 'ln_g', 'ln_b')}
    del _L0_xattn_all

    def _L1_xattn_setup():
        import jax, jax.numpy as jnp
        import numpy as np
        EPS = 1e-05

        def _layernorm(x, g, b):
            m = jnp.mean(x, axis=-1, keepdims=True)
            v = jnp.mean((x - m) ** 2, axis=-1, keepdims=True)
            return (x - m) / jnp.sqrt(v + EPS) * g + b

        def _mha(x, kv, Wq, Wk, Wv, mask, causal):
            m = mask[:, None]
            Q = jnp.einsum('bsd,hdk->bhsk', x, Wq) * m
            K = jnp.einsum('bsd,hdk->bhsk', kv, Wk) * m
            V = jnp.einsum('bsd,hdk->bhsk', kv, Wv) * m
            energy = jnp.einsum('bhsk,bhtk->bhst', Q, K)
            S = energy.shape[-1]
            lengths = jnp.sum(energy[:, :, 0, :] != 0, axis=-1)
            cols = jnp.arange(S)
            energy = jnp.where(cols[None, None, None, :] >= lengths[:, :, None, None], -jnp.inf, energy)
            if causal:
                energy = jnp.where(cols[None, :] > cols[:, None], -jnp.inf, energy)
            dk = Wq.shape[-1]
            score = jax.nn.softmax(energy / jnp.sqrt(jnp.asarray(dk, energy.dtype)), axis=-1)
            out = jnp.einsum('bhst,bhtk->bhsk', score, V) * m
            B, H, Sx, dkk = out.shape
            return out.transpose(0, 2, 1, 3).reshape(B, Sx, H * dkk)
        key = jax.random.key(seed)
        ks = jax.random.split(key, 20)
        B, S, D, H = (2, 512, 256, 16)
        dk = D // H
        sd = 0.02
        inp = {'x': jax.random.normal(ks[0], (B, S, D), jnp.float32), 'context': jax.random.normal(ks[1], (B, S, D), jnp.float32), 'Wq1': jax.random.normal(ks[2], (H, D, dk), jnp.float32) * sd, 'Wk1': jax.random.normal(ks[3], (H, D, dk), jnp.float32) * sd, 'Wv1': jax.random.normal(ks[4], (H, D, dk), jnp.float32) * sd, 'Wq2': jax.random.normal(ks[5], (H, D, dk), jnp.float32) * sd, 'Wk2': jax.random.normal(ks[6], (H, D, dk), jnp.float32) * sd, 'Wv2': jax.random.normal(ks[7], (H, D, dk), jnp.float32) * sd, 'ln1_g': jnp.ones((D,), jnp.float32), 'ln1_b': jnp.zeros((D,), jnp.float32), 'ln2_g': jnp.ones((D,), jnp.float32), 'ln2_b': jnp.zeros((D,), jnp.float32), 'ln3_g': jnp.ones((D,), jnp.float32), 'ln3_b': jnp.zeros((D,), jnp.float32), 'fc1_w': jax.random.normal(ks[8], (D, D), jnp.float32) * sd, 'fc1_b': jnp.zeros((D,), jnp.float32), 'fc2_w': jax.random.normal(ks[9], (D, D), jnp.float32) * sd, 'fc2_b': jnp.zeros((D,), jnp.float32)}
        return inp
    _L1_xattn_all = _L1_xattn_setup()
    _L1_xattn_in = {k: v for k, v in _L1_xattn_all.items() if k in ('Wq1', 'Wk1', 'Wv1', 'Wq2', 'Wk2', 'Wv2', 'ln1_g', 'ln1_b', 'ln2_g', 'ln2_b', 'ln3_g', 'ln3_b', 'fc1_w', 'fc1_b', 'fc2_w', 'fc2_b')}
    del _L1_xattn_all
    return {'x': x, 'ctx_1024': ctx_1024, 'fside_Bx16xSxS2_0': fside_Bx16xSxS2_0, 'L0_xattn_wq': _L0_xattn_in['wq'], 'L0_xattn_bq': _L0_xattn_in['bq'], 'L0_xattn_wk': _L0_xattn_in['wk'], 'L0_xattn_bk': _L0_xattn_in['bk'], 'L0_xattn_wv': _L0_xattn_in['wv'], 'L0_xattn_bv': _L0_xattn_in['bv'], 'L0_xattn_wo': _L0_xattn_in['wo'], 'L0_xattn_bo': _L0_xattn_in['bo'], 'L0_xattn_ln_g': _L0_xattn_in['ln_g'], 'L0_xattn_ln_b': _L0_xattn_in['ln_b'], 'L1_xattn_Wq1': _L1_xattn_in['Wq1'], 'L1_xattn_Wk1': _L1_xattn_in['Wk1'], 'L1_xattn_Wv1': _L1_xattn_in['Wv1'], 'L1_xattn_Wq2': _L1_xattn_in['Wq2'], 'L1_xattn_Wk2': _L1_xattn_in['Wk2'], 'L1_xattn_Wv2': _L1_xattn_in['Wv2'], 'L1_xattn_ln1_g': _L1_xattn_in['ln1_g'], 'L1_xattn_ln1_b': _L1_xattn_in['ln1_b'], 'L1_xattn_ln2_g': _L1_xattn_in['ln2_g'], 'L1_xattn_ln2_b': _L1_xattn_in['ln2_b'], 'L1_xattn_ln3_g': _L1_xattn_in['ln3_g'], 'L1_xattn_ln3_b': _L1_xattn_in['ln3_b'], 'L1_xattn_fc1_w': _L1_xattn_in['fc1_w'], 'L1_xattn_fc1_b': _L1_xattn_in['fc1_b'], 'L1_xattn_fc2_w': _L1_xattn_in['fc2_w'], 'L1_xattn_fc2_b': _L1_xattn_in['fc2_b']}

def reference(x, ctx_1024, fside_Bx16xSxS2_0, L0_xattn_wq, L0_xattn_bq, L0_xattn_wk, L0_xattn_bk, L0_xattn_wv, L0_xattn_bv, L0_xattn_wo, L0_xattn_bo, L0_xattn_ln_g, L0_xattn_ln_b, L1_xattn_Wq1, L1_xattn_Wk1, L1_xattn_Wv1, L1_xattn_Wq2, L1_xattn_Wk2, L1_xattn_Wv2, L1_xattn_ln1_g, L1_xattn_ln1_b, L1_xattn_ln2_g, L1_xattn_ln2_b, L1_xattn_ln3_g, L1_xattn_ln3_b, L1_xattn_fc1_w, L1_xattn_fc1_b, L1_xattn_fc2_w, L1_xattn_fc2_b):
    import jax
    import jax.numpy as jnp

    def _L0_xattn_ref(q, k, v, bias, graph_attn_bias, wq, bq, wk, bk, wv, bv, wo, bo, ln_g, ln_b):
        import jax, jax.numpy as jnp
        import numpy as np
        N_HEADS = 16
        D_MODEL = 256
        D_K = 64
        D_V = 64
        LN_EPS = 1e-06
        B, Lq, D = q.shape
        H, dk, dv = (N_HEADS, D_K, D_V)
        residual = q
        qh = (q @ wq + bq).reshape(B, Lq, H, dk).transpose(0, 2, 1, 3)
        kh = (k @ wk + bk).reshape(B, k.shape[1], H, dk).transpose(0, 2, 1, 3)
        vh = (v @ wv + bv).reshape(B, v.shape[1], H, dv).transpose(0, 2, 1, 3)
        scores = jnp.einsum('bhqd,bhkd->bhqk', qh / np.sqrt(dk).astype(qh.dtype), kh)
        scores = scores + bias + graph_attn_bias
        weights = jax.nn.softmax(scores, axis=-1)
        ctx = jnp.einsum('bhqk,bhkd->bhqd', weights, vh)
        ctx = ctx.transpose(0, 2, 1, 3).reshape(B, Lq, H * dv)
        out = ctx @ wo + bo + residual
        mu = jnp.mean(out, axis=-1, keepdims=True)
        var = jnp.var(out, axis=-1, keepdims=True)
        out = (out - mu) * jax.lax.rsqrt(var + LN_EPS) * ln_g + ln_b
        return out

    def _L1_xattn_ref(x, context, Wq1, Wk1, Wv1, Wq2, Wk2, Wv2, ln1_g, ln1_b, ln2_g, ln2_b, ln3_g, ln3_b, fc1_w, fc1_b, fc2_w, fc2_b):
        import jax, jax.numpy as jnp
        import numpy as np
        EPS = 1e-05

        def _layernorm(x, g, b):
            m = jnp.mean(x, axis=-1, keepdims=True)
            v = jnp.mean((x - m) ** 2, axis=-1, keepdims=True)
            return (x - m) / jnp.sqrt(v + EPS) * g + b

        def _mha(x, kv, Wq, Wk, Wv, mask, causal):
            m = mask[:, None]
            Q = jnp.einsum('bsd,hdk->bhsk', x, Wq) * m
            K = jnp.einsum('bsd,hdk->bhsk', kv, Wk) * m
            V = jnp.einsum('bsd,hdk->bhsk', kv, Wv) * m
            energy = jnp.einsum('bhsk,bhtk->bhst', Q, K)
            S = energy.shape[-1]
            lengths = jnp.sum(energy[:, :, 0, :] != 0, axis=-1)
            cols = jnp.arange(S)
            energy = jnp.where(cols[None, None, None, :] >= lengths[:, :, None, None], -jnp.inf, energy)
            if causal:
                energy = jnp.where(cols[None, :] > cols[:, None], -jnp.inf, energy)
            dk = Wq.shape[-1]
            score = jax.nn.softmax(energy / jnp.sqrt(jnp.asarray(dk, energy.dtype)), axis=-1)
            out = jnp.einsum('bhst,bhtk->bhsk', score, V) * m
            B, H, Sx, dkk = out.shape
            return out.transpose(0, 2, 1, 3).reshape(B, Sx, H * dkk)
        mask0 = 1.0 - jnp.all(x == 0, axis=2, keepdims=True).astype(x.dtype)
        z = _mha(x, x, Wq1, Wk1, Wv1, mask0, causal=True)
        x1 = _layernorm(x + z, ln1_g, ln1_b)
        mask1 = 1.0 - jnp.all(x1 == 0, axis=2, keepdims=True).astype(x1.dtype)
        z = _mha(x1, context, Wq2, Wk2, Wv2, mask1, causal=False)
        x2 = _layernorm(x1 + z, ln2_g, ln2_b)
        z = jnp.maximum(x2 @ fc1_w.T + fc1_b, 0.0) * mask0
        z = (z @ fc2_w.T + fc2_b) * mask0
        return _layernorm(x2 + z, ln3_g, ln3_b)
    x = _L0_xattn_ref(x, ctx_1024, ctx_1024, fside_Bx16xSxS2_0, fside_Bx16xSxS2_0, L0_xattn_wq, L0_xattn_bq, L0_xattn_wk, L0_xattn_bk, L0_xattn_wv, L0_xattn_bv, L0_xattn_wo, L0_xattn_bo, L0_xattn_ln_g, L0_xattn_ln_b)
    x = _L1_xattn_ref(x, ctx_1024, L1_xattn_Wq1, L1_xattn_Wk1, L1_xattn_Wv1, L1_xattn_Wq2, L1_xattn_Wk2, L1_xattn_Wv2, L1_xattn_ln1_g, L1_xattn_ln1_b, L1_xattn_ln2_g, L1_xattn_ln2_b, L1_xattn_ln3_g, L1_xattn_ln3_b, L1_xattn_fc1_w, L1_xattn_fc1_b, L1_xattn_fc2_w, L1_xattn_fc2_b)
    return x

_drawn_inputs = setup_inputs


def setup_inputs(seed=0):
    import zlib

    import numpy as np

    out = dict(_drawn_inputs(seed))
    spreads = {'L0_xattn_bq': (0.0, 0.1),
     'L0_xattn_bk': (0.0, 0.8),
     'L0_xattn_bv': (0.0, 0.1),
     'L0_xattn_bo': (0.0, 0.1),
     'L0_xattn_ln_g': (1.0, 0.2),
     'L0_xattn_ln_b': (0.0, 0.1),
     'L1_xattn_ln1_g': (1.0, 0.2),
     'L1_xattn_ln1_b': (0.0, 0.1),
     'L1_xattn_ln2_g': (1.0, 0.2),
     'L1_xattn_ln2_b': (0.0, 0.1),
     'L1_xattn_ln3_g': (1.0, 0.2),
     'L1_xattn_ln3_b': (0.0, 0.1),
     'L1_xattn_fc1_b': (0.0, 0.356),
     'L1_xattn_fc2_b': (0.0, 0.1)}
    factors = {'L1_xattn_Wq1': 8.0, 'L1_xattn_Wk1': 8.0, 'L1_xattn_Wq2': 8.0, 'L1_xattn_Wk2': 8.0}
    for name, (base, spread) in spreads.items():
        noise = np.random.default_rng([zlib.crc32(name.encode()), seed]).standard_normal(out[name].shape)
        drawn = base * np.exp(spread * noise) if base else spread * noise
        out[name] = jnp.asarray(drawn.astype(out[name].dtype))
    for name, factor in factors.items():
        out[name] = (out[name] * factor).astype(out[name].dtype)
    return out
```

```python
from contextlib import ExitStack

import numpy as np

import concourse.bass as bass
from concourse import mybir

P = 128
F32 = mybir.dt.float32
F32R = mybir.dt.float32r
BF16 = mybir.dt.bfloat16
I32 = mybir.dt.int32
ALU = mybir.AluOpType
ACT = mybir.ActivationFunctionType
AX = mybir.AxisListType

BIG = 1.0e30
LN_EPS0 = 1e-6
LN_EPS1 = 1e-5
DVE_STEPS = 82

WORK = (["xT", "cT"] + [f"q{n}" for n in range(4)] + [f"k{n}" for n in range(4)] + [f"v{n}" for n in range(4)]
        + [f"pv{n}" for n in range(8)] + [f"ct{n}" for n in range(4)]
        + [f"a.{n}" for n in ("T", "q", "k", "e0", "len", "v", "mT", "pv0", "pv1", "z0", "z1")]
        + [f"b.{n}" for n in ("T", "cT", "q", "k", "e0", "len", "v", "mT", "pv0", "pv1", "z0", "z1")]
        + [f"f.{n}" for n in ("T", "h", "o")])
WORK_PER_BANK = len(WORK) // 2
assert len(WORK) == 2 * WORK_PER_BANK


def build(nc, x, ctx_in, fside, w0, vec0, w1, vec1, out):
    B, S, D = x.shape
    H = fside.shape[1]
    DK0 = 64
    DK1 = D // H
    C = D // P
    NP = H // 2
    E0 = H * DK0
    DV = DK0 + 1
    SPLIT = 3 * DK1
    assert S == 2 * P and C == 2 and H == 16 and DK1 == 16

    stack = ExitStack()
    with stack:
        def sb(name, shape, dt=F32):
            return stack.enter_context(nc.sbuf_tensor(name, shape, dt))

        def sem(name):
            return stack.enter_context(nc.semaphore(name))

        W0 = {n: [sb(f"w0{n}_{p}", [P, C, E0], F32R) for p in ("hi", "lo")] for n in "qkv"}
        Wo = [sb(f"w0o_{p}", [P, E0 // P, D], F32R) for p in ("hi", "lo")]
        W1 = {n: [sb(f"w1{n}_{p}", [P, C, D], F32R) for p in ("hi", "lo")] for n in w1}
        bv_col = sb("bv_col", [P, E0 // P])
        bv_parts = [sb(f"bv_{p}", [P, E0 // P], F32R) for p in ("hi", "lo")]
        rows = sb("rows", [P, len(vec1), D])
        row = {n: rows[:, k, :] for k, n in enumerate(vec1)}
        bq_col = sb("bq_col", [P, NP])
        bk_col = sb("bk_col", [P, NP])
        fb_col = sb("fb_col", [P, C])
        ident = sb("ident", [P, P])
        identb = sb("identb", [P, P], BF16)
        ones = sb("ones", [P, P])
        mask_q = sb("mask_q", [P, 2 * P], BF16)
        mask_k = sb("mask_k", [P, 2 * P], BF16)
        blk = sb("blk", [P, P])
        sel = sb("sel", [P, P // DK1])
        key_row = sb("key_row", [P, S])
        key_col = sb("key_col", [P, 2])
        neg_half = sb("neg_half", [P, 2])
        x_nat = sb("x_nat", [P, 2, D])
        c_nat = sb("c_nat", [P, 2, D])
        T1 = [sb(f"T1_{p}", [P, C, S], F32R) for p in ("hi", "lo")]
        T2 = [sb(f"T2_{p}", [P, C, S], F32R) for p in ("hi", "lo")]
        QZ0 = sb("QZ0", [P, 2, NP, S])
        KT0 = sb("KT0", [P, NP, S])
        V0 = sb("V0", [P, 2, H, DV])
        NR = 4
        ring = sb("ring", [P, NR, 2, 2, S])
        low = sb("low", [P, NR, 2, 2])
        PT = sb("PT", [P, 2, 2, 2, S])
        stage = sb("stage", [P, 2048])
        ctx_cat = stage[:, :].rearrange("p (h e) -> p h e", h=2)
        parts = stage[:, :].rearrange("p (w s g t) -> p w s g t", w=2, s=2, g=2)
        z_raw = stage[:, 0:4 * S].rearrange("p (u t) -> p u t", u=4)
        rec0 = sb("rec0", [P, 2, 2])
        cur = sb("cur", [P, 2, D])
        tmp = sb("tmp", [P, 2, D])
        K1 = x_nat[:, :, :]
        QS1 = sb("QS1", [P, NP, S], F32R)
        KS1 = sb("KS1", [P, NP, S], F32R)
        V1 = V0[:, :, :, 0:32]
        q0c = sb("q0c", [P, 2])
        k0c = sb("k0c", [P, 2])
        junk = tmp[:, 0, :]
        Q0blk = tmp[:, 1, :].rearrange("p (g c) -> p g c", g=2)
        drop = tmp[:, :, :].bitcast(I32)
        max_row = tmp[0:H, 0, :].bitcast(F32R)
        length = sb("length", [P, 2])
        sel_len = sb("sel_len", [P, H])
        keep = sb("keep", [P, 2, H])
        neg_max = sb("neg_max", [P, 2, H])
        mask0 = sb("mask0", [P, 2])
        mask1 = sb("mask1", [P, 2])
        rec1 = sb("rec1", [P, H])
        st = sb("st", [P, 2, 6])
        mv = sb("mv", [P, 2, 2])
        veps = sb("veps", [P, 2])
        rstd = sb("rstd", [P, 2])
        carrier = sb("carrier", [P, 64])

        A = [stack.enter_context(nc.psum_tensor(f"A{n}", [P, 512], F32)) for n in range(2)]
        SC = [stack.enter_context(nc.psum_tensor(f"SC{n}", [P, 2, 2, S], F32)) for n in range(2)]
        W = [stack.enter_context(nc.psum_tensor(f"W{n}", [P, 512], F32)) for n in range(2)]
        A_USES = 3 * NP + 1

        weights_in = [sem(f"weights_in{n}") for n in range(2)]
        vectors_in = sem("vectors_in")
        hi_ready = sem("hi_ready")
        bv_step = sem("bv_step")
        bvo_full = sem("bvo_full")
        bo_ready = sem("bo_ready")
        split_ready = sem("split_ready")
        consts_ready = sem("consts_ready")
        pool_step = sem("pool_step")
        x_in = sem("x_in")
        c_in = sem("c_in")
        bias_in = [sem(f"bias_in{n}") for n in range(NR)]
        xb_ready = sem("xb_ready")
        work_full = [sem(f"work_full{n}") for n in range(2)]
        work_free = [sem(f"work_free{n}") for n in range(2)]
        a_full = [sem(f"a_full{n}") for n in range(2)]
        a_free = [sem(f"a_free{n}") for n in range(2)]
        shifted = sem("shifted")
        sc_full = sem("sc_full")
        exp_done = sem("exp_done")
        pv_done = sem("pv_done")
        stats_ready = sem("stats_ready")
        rstd_ready = sem("rstd_ready")
        norm_done = sem("norm_done")
        cm_ready = sem("cm_ready")
        q0_ready = sem("q0_ready")
        q0blk_ready = sem("q0blk_ready")
        len_ready = sem("len_ready")
        sel_ready = sem("sel_ready")
        k1_ready = sem("k1_ready")
        qhi_ready = sem("qhi_ready")
        khi_ready = sem("khi_ready")
        k_parts = sem("k_parts")
        scr_in = sem("scr_in")
        stacks_in = sem("stacks_in")
        v1_ready = sem("v1_ready")
        max_out = sem("max_out")
        max_in = sem("max_in")
        c_used = sem("c_used")
        ring_free = sem("ring_free")
        out_stored = sem("out_stored")
        dve_step = sem("dve_step")

        scratch = nc.dram_tensor("scratch", [2, 2, 2, P, S], F32).ap()

        max_scratch = nc.dram_tensor("max_scratch", [H, S], F32).ap()

        SCALE0 = 0.5 / float(DK0) ** 0.5
        SCALE1 = 1.0 / float(DK1) ** 0.5

        PV_DONES = NP - 2

        def work(name):
            n = WORK.index(name)
            return n % 2, n // 2

        def wait_work_free(eng, i, name):
            b, k = work(name)
            eng.wait_ge(work_free[b], i * WORK_PER_BANK + k)
            return W[b]

        def wait_work_full(eng, i, name):
            b, k = work(name)
            eng.wait_ge(work_full[b], i * WORK_PER_BANK + k + 1)
            return W[b]

        def wait_read(eng, i, name):
            b, k = work(name)
            eng.wait_ge(work_free[b], i * WORK_PER_BANK + k + 1)

        carriers = []

        def part_wait(eng):
            column = carrier[:, len(carriers):len(carriers) + 1]
            carriers.append(column)
            if eng.engine == nc.vector.engine:
                nc.vector.memset(column, 0.0)
            else:
                nc.gpsimd.tensor_tensor(column, neg_half[:, 0:1], neg_half[:, 0:1], ALU.add)

        def filled(ins, name):
            return ins.then_inc(work_full[work(name)[0]], 1)

        def freed(ins, name):
            return ins.then_inc(work_free[work(name)[0]], 1)

        bv_wide = [T[:, 0:4, :].rearrange("p j (e c) -> p (j e) c", e=2) for T in (QS1, KS1)]
        weight_list = ([(w0[n], W0[n]) for n in "qkv"] + [(w0["o"], Wo)] + [(w1[n], W1[n]) for n in w1])
        ring_flat = ring[:, :, :, :, :].rearrange("p n a b s -> p (n a b s)")
        STG = 2048

        def staging(n):
            cols = weight_list[n][0].shape[0] // P * weight_list[n][0].shape[1]
            return ring_flat[:, (n % 2) * STG:(n % 2) * STG + cols], cols

        block = stack.enter_context(nc.Block())

        @block.sync
        def _(sp):
            for n, (dram, _) in enumerate(weight_list):
                if n >= 2:
                    sp.wait_ge(split_ready, n - 1)
                dst, cols = staging(n)
                sp.dma_start(dst.rearrange("p (c n) -> p c n", n=dram.shape[1]),
                             dram.rearrange("(c p) n -> p c n", p=P)).then_inc(weights_in[n % 2], 16)
                if n == 0:
                    nvec = 0
                    for dst_v, src_v in [(bv_col[:, :], vec0["bv"].rearrange("(j r) -> r j", r=P)),
                                         (bq_col[:, :], vec0["bq"].rearrange("(j r) -> r j", r=P)),
                                         (bk_col[:, :], vec0["bk"].rearrange("(j r) -> r j", r=P)),
                                         (fb_col[:, :], vec0["fb"].rearrange("(j r) -> r j", r=P))] + [
                                             (row[m], vec1[m].partition_broadcast(P)) for m in vec1]:
                        sp.dma_start(dst_v, src_v, allow_slow_non_contiguous=True).then_inc(vectors_in, 16)
                        nvec += 1
            sp.wait_ge(split_ready, len(weight_list))
            with sp.Fori(0, B) as i:
                sp.wait_ge(v1_ready, 2 * i)
                sp.dma_start(x_nat[:, :, :], x[i].rearrange("(h p) d -> p h d", p=P)).then_inc(x_in, 16)
                sp.wait_ge(c_used, i)
                sp.dma_start(c_nat[:, :, :], ctx_in[i].rearrange("(h p) d -> p h d", p=P)).then_inc(c_in, 16)
                for p in range(NP):
                    if p < NR:
                        sp.wait_ge(ring_free, NP * i)
                    else:
                        sp.wait_ge(ring_free, NP * i + p - NR + 1)
                    sp.dma_start(ring[:, p % NR], fside[i, 2 * p:2 * p + 2].rearrange("a (h q) k -> q a h k", q=P))\
                        .then_inc(bias_in[p % NR], 16)
            sp.wait_ge(out_stored, 16 * B)

        @block.gpsimd
        def _(pool):
            g = nc.gpsimd
            n = [0]

            def step(ins):
                n[0] += 1
                ins.then_inc(pool_step, 1)
                pool.wait_ge(pool_step, n[0])

            step(g.memset(ones[:, :], 1.0))
            step(g.memset(ident[:, :], 0.0))
            step(g.affine_select(out=ident[:, :], in_=ident[:, :], compare_op=ALU.not_equal, fill=1.0,
                                 base=0, pattern=[[-1, P]], channel_multiplier=1))
            step(g.tensor_copy(identb[:, :], ident[:, :]))
            step(g.memset(mask_q[:, :], -BIG))
            step(g.memset(mask_k[:, :], -BIG))
            step(g.affine_select(out=mask_q[:, 0:P], in_=mask_q[:, 0:P], compare_op=ALU.is_gt, fill=0.0,
                                 base=0, pattern=[[1, P]], channel_multiplier=-1))
            step(g.affine_select(out=mask_k[:, P:2 * P], in_=mask_k[:, P:2 * P], compare_op=ALU.is_gt, fill=0.0,
                                 base=0, pattern=[[-1, P]], channel_multiplier=1))
            for t, inner in ((blk, [[0, DK1]]), (sel, [])):
                v = t[:, :].rearrange("p (j d) -> p j d", d=DK1) if inner else t[:, :]
                step(g.memset(t[:, :], 1.0 if inner else 1.0 / DK1))
                step(g.affine_select(out=v, in_=v, compare_op=ALU.is_ge, fill=0.0, base=0,
                                     pattern=[[-DK1, P // DK1]] + inner, channel_multiplier=1))
                step(g.affine_select(out=v, in_=v, compare_op=ALU.is_ge, fill=0.0, base=DK1 - 1,
                                     pattern=[[DK1, P // DK1]] + inner, channel_multiplier=-1))
            step(g.iota(drop[:, 0], [[1, S]], base=0, channel_multiplier=0))
            step(g.tensor_copy(key_row[:, :], drop[:, 0]))
            step(g.iota(drop[:, 0, 0:2], [[P, 2]], base=0, channel_multiplier=1))
            step(g.tensor_copy(key_col[:, :], drop[:, 0, 0:2]))
            step(g.memset(neg_half[:, :], -0.5))
            step(g.memset(QZ0[:, :, :, :], 0.0))
            step(g.memset(V0[:, :, :, DK0:DV], 1.0))
            pool.wait_ge(vectors_in, 16 * (4 + len(vec1)))
            g.tensor_scalar(bq_col[:, :], bq_col[:, :], SCALE0, 1.0, ALU.mult, ALU.mult).then_inc(consts_ready, 1)

            pool.wait_ge(bo_ready, 1)
            step(g.memset(KS1[:, :, :].bitcast(F32), 1.0))
            with pool.Fori(0, B) as i:
                wait_work_full(pool, i, "xT")
                for h in range(2):
                    ins = g.tensor_tensor(x_nat[:, h], x_nat[:, h], row["bo"], ALU.add)
                ins.then_inc(xb_ready, 1)
                for h in range(H):
                    pool.wait_ge(a_free[h % 2], A_USES * i + h // 2 + 1)
                    part_wait(pool)
                    for qh in range(2):
                        s = ring[:, (h // 2) % NR, h % 2, qh]
                        ins = g.tensor_scalar(s, s, -1.0, low[:, (h // 2) % NR, h % 2, qh:qh + 1], ALU.mult, ALU.add)
                    ins.then_inc(shifted, 1)

                def power(k, eps):
                    pool.wait_ge(stats_ready, 4 * i + k + 1)
                    part_wait(pool)
                    g.tensor_scalar(veps[:, :], mv[:, :, 1], eps, 1.0, ALU.add, ALU.mult).then_inc(pool_step, 1)
                    pool.wait_ge(pool_step, n[0] + 4 * i + k + 1)
                    g.tensor_tensor(rstd[:, :], veps[:, :], neg_half[:, :], ALU.pow).then_inc(rstd_ready, 1)

                def decoder(m):
                    pool.wait_ge(q0_ready, 2 * i + m + 1)
                    part_wait(pool)
                    for gr in range(2):
                        ins = g.tensor_scalar(Q0blk[:, gr], blk[:, :], q0c[:, gr:gr + 1], 1.0, ALU.mult, ALU.mult)
                    ins.then_inc(q0blk_ready, 1)

                power(0, LN_EPS0)
                decoder(0)
                power(1, LN_EPS1)
                decoder(1)
                power(2, LN_EPS1)
                power(3, LN_EPS1)

        @block.scalar
        def _(act):
            s = nc.scalar
            for n, (_, (hi, lo)) in enumerate(weight_list):
                act.wait_ge(weights_in[n % 2], 16 * (n // 2 + 1))
                src, cols = staging(n)
                s.activation(hi[:, :, :].rearrange("p c n -> p (c n)"), src, ACT.Copy).then_inc(hi_ready, 1)
            act.wait_ge(consts_ready, 1)

            with act.Fori(0, B) as i:
                for u in range(4):
                    w = wait_work_full(act, i, f"k{u}")
                    for v in range(2):
                        ins = s.activation(KT0[:, 2 * u + v], w[:, v * S:(v + 1) * S], ACT.Identity,
                                           bias=bk_col[:, 2 * u + v:2 * u + v + 1])
                    freed(ins, f"k{u}")

                for u in range(4):
                    w = wait_work_full(act, i, f"v{u}")
                    freed(s.activation(V0[:, u // 2, 8 * (u % 2):8 * (u % 2) + 8, 0:DK0],
                                       w[:, :].rearrange("p (h d) -> p h d", d=DK0), ACT.Copy), f"v{u}")

                def exps(layer, scale):
                    for p in range(NP):
                        act.wait_ge(sc_full, 3 * NP * i + NP * layer + p + 1)
                        if p >= 2 and layer == 0:
                            wait_work_full(act, i, f"pv{p - 2}")
                        elif p >= 2 and (p - 2) % 4 == 3:
                            wait_work_full(act, i, f"{'ab'[layer - 1]}.pv{(p - 2) // 4}")
                        elif p >= 2:
                            act.wait_ge(pv_done, PV_DONES * (2 * i + layer - 1) + p - 1 - (p - 1) // 4)
                        s.activation(PT[:, p % 2], SC[p % 2][:, :, :, :], ACT.Exp, scale=scale).then_inc(exp_done, 1)

                exps(0, 2.0)

                def decoder(m):
                    t = "ab"[m]
                    w = wait_work_full(act, i, f"{t}.q")
                    s.activation(parts[:, 0, 0].bitcast(F32R), w[:, :].rearrange("p (g t) -> p g t", g=2), ACT.Copy)\
                        .then_inc(qhi_ready, 1)
                    w = wait_work_full(act, i, f"{t}.k")
                    freed(s.activation(K1, w[:, :].rearrange("p (g t) -> p g t", g=2), ACT.Copy), f"{t}.k")
                    wait_read(act, i, f"{t}.q")
                    act.dma_start(scratch[0].rearrange("s g p t -> p s g t"), parts[:, 0]).then_inc(scr_in, 16)
                    act.wait_ge(k1_ready, 2 * i + m + 1)
                    s.activation(parts[:, 1, 0].bitcast(F32R), K1, ACT.Copy).then_inc(khi_ready, 1)
                    act.wait_ge(scr_in, 32 * (2 * i + m) + 16)
                    for gr in range(2):
                        for c, part in enumerate((0, 1, 0)):
                            act.dma_start(QS1[64 * gr + DK1 * c:64 * gr + DK1 * (c + 1)].bitcast(F32),
                                          scratch[0, part, gr].rearrange("(j d) t -> d j t", d=DK1))\
                                .then_inc(stacks_in, 16)
                    for r in range(2):
                        act.dma_start(QS1[64 * r + SPLIT:64 * r + SPLIT + 1].bitcast(F32),
                                      QZ0[DK0:DK0 + 1, 0]).then_inc(stacks_in, 16)
                    act.wait_ge(k_parts, 2 * i + m + 1)
                    act.dma_start(scratch[1].rearrange("s g p t -> p s g t"), parts[:, 1]).then_inc(scr_in, 16)
                    act.wait_ge(scr_in, 32 * (2 * i + m) + 32)
                    for gr in range(2):
                        for c, part in enumerate((0, 0, 1)):
                            act.dma_start(KS1[64 * gr + DK1 * c:64 * gr + DK1 * (c + 1)].bitcast(F32),
                                          scratch[1, part, gr].rearrange("(j d) t -> d j t", d=DK1))\
                                .then_inc(stacks_in, 16)
                    wait_read(act, i, f"{t}.mT")
                    act.dma_start(max_scratch, max_row.bitcast(F32)).then_inc(max_out, 16)
                    act.wait_ge(max_out, 16 * (2 * i + m + 1))
                    for gr in range(2):
                        act.dma_start(QS1[64 * gr + SPLIT:64 * gr + SPLIT + 1].bitcast(F32),
                                      max_scratch[NP * gr:NP * (gr + 1), :].unsqueeze(0)).then_inc(max_in, 16)
                    exps(1 + m, SCALE1)
                    for u in range(2):
                        w = wait_work_full(act, i, f"{t}.pv{u}")
                        freed(s.activation(z_raw[:, 2 * u:2 * u + 2], w[:, :].rearrange("p (v t) -> p v t", v=2),
                                                           ACT.Copy), f"{t}.pv{u}")

                decoder(0)
                decoder(1)
                act.wait_ge(norm_done, 4 * i + 4)
                act.dma_start(out[i].rearrange("(h p) d -> p h d", p=P), tmp[:, :, :]).then_inc(out_stored, 16)

        @block.vector
        def _(dve):
            v = nc.vector
            for n, (_, (hi, lo)) in enumerate(weight_list):
                src, cols = staging(n)
                dve.wait_ge(hi_ready, n + 1)
                v.tensor_tensor(lo[:, :, :].rearrange("p c n -> p (c n)"), src,
                                hi[:, :, :].rearrange("p c n -> p (c n)").bitcast(F32), ALU.subtract)\
                    .then_inc(split_ready, 1)
            dve.wait_ge(consts_ready, 1)
            v.tensor_copy(bv_parts[0][:, :], bv_col[:, :]).then_inc(bv_step, 1)
            dve.wait_ge(bv_step, 1)
            v.tensor_tensor(bv_parts[1][:, :], bv_col[:, :], bv_parts[0][:, :].bitcast(F32), ALU.subtract)\
                .then_inc(bv_step, 1)
            dve.wait_ge(bv_step, 2)
            for k in range(2):
                for j in range(E0 // P):
                    ins = v.tensor_copy(bv_wide[k][:, j, :],
                                        bv_parts[k][:, j:j + 1].bitcast(F32).broadcast_to([P, P]))
            ins.then_inc(bv_step, 1)
            dve.wait_ge(bvo_full, 1)
            v.tensor_tensor(row["bo"], row["bo"], A[0][:, 0:D], ALU.add).then_inc(bo_ready, 1)
            STEPS = DVE_STEPS
            with dve.Fori(0, B) as i:
                done = [0]

                def step(ins):
                    ins.then_inc(dve_step, 1)
                    done[0] += 1
                    dve.wait_ge(dve_step, STEPS * i + done[0])

                def split(T, name):
                    w = wait_work_full(dve, i, name)[:, :].rearrange("p (c t) -> p c t", c=C)
                    step(v.tensor_copy(T[0][:, :, :], w))
                    return freed(v.tensor_tensor(T[1][:, :, :], w, T[0][:, :, :].bitcast(F32), ALU.subtract), name)

                def layer_norm(src, k, gain, bias):
                    for h in range(2):
                        ins = v.bn_stats(st[:, h], src[:, h])
                        step(ins)
                    part_wait(dve)
                    for h in range(2):
                        ins = v.bn_aggr(mv[:, h], st[:, h])
                        if h == 0:
                            ins.then_inc(dve_step, 1)
                            done[0] += 1
                        else:
                            ins.then_inc(stats_ready, 1)
                    dve.wait_ge(dve_step, STEPS * i + done[0])
                    dve.wait_ge(rstd_ready, 4 * i + k + 1)
                    for h in range(2):
                        step(v.tensor_scalar(src[:, h], src[:, h], mv[:, h, 0:1], rstd[:, h:h + 1],
                                             ALU.subtract, ALU.mult))
                    for h in range(2):
                        step(v.tensor_tensor(src[:, h], src[:, h], row[gain], ALU.mult))
                    dst = tmp if k == 3 else cur
                    if k == 3:
                        dve.wait_ge(out_stored, 16 * i)
                    for h in range(2):
                        ins = v.tensor_tensor(dst[:, h], src[:, h], row[bias], ALU.add)
                        if h == 0:
                            ins.then_inc(dve_step, 1)
                            done[0] += 1
                        else:
                            ins.then_inc(norm_done, 1)
                    dve.wait_ge(dve_step, STEPS * i + done[0])
                    dve.wait_ge(norm_done, 4 * i + k + 1)

                split(T1, "xT")
                split(T2, "cT")
                for u in range(4):
                    w = wait_work_full(dve, i, f"q{u}")[:, :].rearrange("p (v t) -> p v t", v=2)
                    for a in range(2):
                        r = slice(64 * a, 64 * a + 64)
                        ins = v.scalar_tensor_tensor(
                            QZ0[r, a, 2 * u:2 * u + 2], w[r], SCALE0,
                            bq_col[r, 2 * u:2 * u + 2].unsqueeze(2).broadcast_to([64, 2, S]), ALU.mult, ALU.add)
                    freed(ins, f"q{u}")

                def score(p):
                    slot = p % NR
                    dve.wait_ge(bias_in[slot], 16 * (NP // NR) * i + 16 * (p // NR) + 16)
                    for a in range(2):
                        dve.wait_ge(a_full[a], A_USES * i + p + 1)
                        part_wait(dve)
                        for qh in range(2):
                            s = ring[:, slot, a, qh]
                            ins = v.tensor_tensor_reduce(out=s, in0=A[a][:, qh * S:(qh + 1) * S], in1=s, scale=-1.0,
                                                         scalar=3.0e38, op0=ALU.add, op1=ALU.min,
                                                         accum_out=low[:, slot, a, qh:qh + 1])
                        ins.then_inc(a_free[a], 1)

                def weigh(p):
                    w = wait_work_full(dve, i, f"pv{p}")[:, 0:4 * DV].rearrange("p (a h e) -> p a h e", a=2, h=2)
                    if p >= 1:
                        wait_read(dve, i, f"pv{p - 1}")
                    step(v.reciprocal(rec0[:, :, :], w[:, :, :, DK0]))
                    freed(v.tensor_tensor(ctx_cat[:, :, P * p:P * (p + 1)].rearrange("p h (a e) -> p a h e", a=2),
                                          w[:, :, :, 0:DK0],
                                          rec0[:, :, :].unsqueeze(3).broadcast_to([P, 2, 2, DK0]), ALU.mult), f"pv{p}")

                for p in range(NP + 2):
                    if p < NP:
                        score(p)
                    if p >= 2:
                        weigh(p - 2)
                for u in range(4):
                    split((T1, T2)[u % 2], f"ct{u}")
                dve.wait_ge(xb_ready, i + 1)
                for h in range(2):
                    dve.wait_ge(a_full[h], A_USES * i + NP + 1)
                    ins = v.tensor_tensor(cur[:, h], A[h][:, 0:D], x_nat[:, h], ALU.add).then_inc(a_free[h], 1)
                    dve.wait_ge(a_free[h], A_USES * i + NP + 1)
                layer_norm(cur, 0, "ln_g", "ln_b")

                def token_mask(mask):
                    for h in range(2):
                        step(v.tensor_scalar(junk, cur[:, h], 0.0, None, ALU.not_equal, ALU.max,
                                             accum_out=mask[:, h:h + 1]))

                def decoder(m):
                    t = "ab"[m]
                    causal = m == 0
                    mask = (mask0, mask1)[m]
                    token_mask(mask)
                    if m == 1:
                        for h in range(2):
                            ins = v.tensor_scalar(c_nat[:, h], c_nat[:, h], mask[:, h:h + 1], 1.0, ALU.mult, ALU.mult)
                        ins.then_inc(cm_ready, 1)
                    split(T1, f"{t}.T")
                    if m == 1:
                        split(T2, f"{t}.cT")
                    w = wait_work_full(dve, i, f"{t}.q")[:, :].rearrange("p (g t) -> p g t", g=2)
                    dve.wait_ge(qhi_ready, 2 * i + m + 1)
                    v.tensor_copy(q0c[:, :], w[:, :, 0]).then_inc(q0_ready, 1)
                    freed(v.tensor_tensor(parts[:, 0, 1].bitcast(F32R), w, parts[:, 0, 0], ALU.subtract), f"{t}.q")
                    w = wait_work_full(dve, i, f"{t}.e0")
                    for gr in range(2):
                        ins = v.tensor_scalar(junk, w[:, gr * S:(gr + 1) * S], 0.0, None, ALU.not_equal,
                                              ALU.add, accum_out=length[:, gr:gr + 1])
                        if gr == 0:
                            step(ins)
                    freed(ins, f"{t}.e0")
                    wait_read(dve, i, f"{t}.e0")
                    for gr in range(2):
                        ins = v.tensor_scalar(sel_len[:, NP * gr:NP * (gr + 1)], sel[:, :], length[:, gr:gr + 1], 1.0,
                                              ALU.mult, ALU.mult)
                    ins.then_inc(sel_ready, 1)
                    wait_read(dve, i, f"{t}.k")
                    step(v.tensor_copy(k0c[:, :], K1[:, :, 0]))
                    for gr in range(2):
                        step(v.tensor_scalar(drop[:, gr], key_row[:, :], length[:, gr:gr + 1], None, ALU.is_ge))
                    part_wait(dve)
                    v.copy_predicated(K1, drop, k0c[:, :].unsqueeze(2).broadcast_to([P, 2, S]))\
                        .then_inc(k1_ready, 1)
                    dve.wait_ge(khi_ready, 2 * i + m + 1)
                    v.tensor_tensor(parts[:, 1, 1].bitcast(F32R), K1, parts[:, 1, 0], ALU.subtract)\
                        .then_inc(k_parts, 1)
                    w = wait_work_full(dve, i, f"{t}.len")
                    for kh in range(2):
                        ins = v.tensor_scalar(keep[:, kh], w[:, 0:H], key_col[:, kh:kh + 1], None, ALU.is_gt)
                        if kh == 0:
                            step(ins)
                    freed(ins, f"{t}.len")
                    wait_read(dve, i, f"{t}.len")
                    w = wait_work_full(dve, i, f"{t}.v")
                    freed(v.tensor_tensor(V0[:, :, :, 0:DK1],
                                          w[:, :].rearrange("p (k h d) -> p k h d", k=2, d=DK1),
                                          keep[:, :, :].unsqueeze(3).broadcast_to([P, 2, H, DK1]), ALU.mult), f"{t}.v")
                    v.tensor_copy(V0[:, :, :, DK1], keep[:, :, :]).then_inc(v1_ready, 1)
                    for p in range(NP):
                        for gr in range(2):
                            dve.wait_ge(a_full[gr], A_USES * i + NP + 1 + NP * m + p + 1)
                            ins = v.tensor_reduce(out=neg_max[:, :, NP * gr + p], in_=A[gr][:, :].rearrange(
                                "p (h t) -> p h t", h=2), axis=AX.X, op=ALU.max, negate=True).then_inc(a_free[gr], 1)
                    w = wait_work_full(dve, i, f"{t}.mT")
                    freed(v.tensor_copy(max_row, w[0:H, 0:S]), f"{t}.mT")
                    for h in range(2):
                        w = wait_work_full(dve, i, f"{t}.z{h}")
                        zz = w[:, :].rearrange("p (u g e) -> p g u e", g=2, e=32)
                        rr = rec1[:, :].rearrange("p (g u) -> p g u", g=2)
                        step(v.reciprocal(rr, zz[:, :, :, DK1]))
                        step(v.tensor_scalar(rec1[:, :], rec1[:, :], mask[:, h:h + 1], 1.0, ALU.mult, ALU.mult))
                        freed(v.tensor_tensor(tmp[:, h].rearrange("p (g u d) -> p g u d", g=2, d=DK1),
                                              zz[:, :, :, 0:DK1],
                                              rr.unsqueeze(3).broadcast_to([P, 2, NP, DK1]), ALU.mult), f"{t}.z{h}")
                        wait_read(dve, i, f"{t}.z{h}")
                        step(v.tensor_tensor(cur[:, h], cur[:, h], tmp[:, h], ALU.add))
                    layer_norm(cur, 1 + m, ("ln1_g", "ln2_g")[m], ("ln1_b", "ln2_b")[m])

                dve.wait_ge(out_stored, 16 * i)
                decoder(0)
                decoder(1)
                split(T1, "f.T")
                w = wait_work_full(dve, i, "f.h")[:, :].rearrange("p (c t) -> p c t", c=C)
                for c in range(C):
                    step(v.tensor_scalar(tmp[:, c], w[:, c], fb_col[:, c:c + 1], 0.0, ALU.add, ALU.max))
                step(v.tensor_copy(T2[0][:, :, :], tmp[:, :, :]))
                freed(v.tensor_tensor(T2[1][:, :, :], tmp[:, :, :], T2[0][:, :, :].bitcast(F32), ALU.subtract), "f.h")
                w = wait_work_full(dve, i, "f.o")[:, :].rearrange("p (h d) -> p h d", h=2)
                for h in range(2):
                    ins = v.tensor_tensor(tmp[:, h], w[:, h], row["fc2_b"], ALU.add)
                    if h == 0:
                        step(ins)
                freed(ins, "f.o")
                wait_read(dve, i, "f.o")
                for h in range(2):
                    step(v.scalar_tensor_tensor(cur[:, h], tmp[:, h], mask0[:, h:h + 1], cur[:, h], ALU.mult, ALU.add))
                layer_norm(cur, 3, "ln3_g", "ln3_b")
                assert done[0] == DVE_STEPS, done[0]

        @block.tensor
        def _(pe):
            t = nc.tensor
            pe.wait_ge(split_ready, len(weight_list))
            pe.wait_ge(consts_ready, 1)

            def product(dst, pairs, start=True):
                terms = [(a[x], b[y]) for a, b in pairs for x, y in ((0, 0), (0, 1), (1, 0))]
                for k, (a, b) in enumerate(terms):
                    ins = t.matmul(dst, a, b, start=start and k == 0, stop=k == len(terms) - 1)
                return ins

            def cut(T, *index):
                return [part[index] for part in T]

            pe.wait_ge(bv_step, 3)
            terms = [(j, a, b) for j in range(E0 // P) for a, b in ((0, 0), (0, 1), (1, 0))]
            for k, (j, a, b) in enumerate(terms):
                ins = t.matmul(A[0][:, 0:D], bv_wide[a][:, j, :], Wo[b][:, j, :], start=k == 0, stop=k == len(terms) - 1)
            ins.then_inc(bvo_full, 1)
            pe.wait_ge(bo_ready, 1)

            with pe.Fori(0, B) as i:
                def transpose4(name, src):
                    w = wait_work_free(pe, i, name)
                    for c in range(C):
                        for h in range(2):
                            ins = t.transpose(w[:, c * S + h * P:c * S + (h + 1) * P], src[:, h, c * P:(c + 1) * P],
                                              ident[:, :])
                    return filled(ins, name)

                def wait_split(name):
                    wait_read(pe, i, name)

                every = slice(None)
                pe.wait_ge(x_in, 16 * i + 16)
                transpose4("xT", x_nat)
                pe.wait_ge(c_in, 16 * i + 16)
                transpose4("cT", c_nat)
                wait_split("xT")
                for u in range(4):
                    w = wait_work_free(pe, i, f"q{u}")
                    for vv in range(2):
                        col = slice((2 * u + vv) * P, (2 * u + vv + 1) * P)
                        ins = product(w[:, vv * S:(vv + 1) * S],
                                      [(cut(W0["q"], every, c, col), cut(T1, every, c, every)) for c in range(C)])
                    filled(ins, f"q{u}")
                wait_split("cT")
                for u in range(4):
                    w = wait_work_free(pe, i, f"k{u}")
                    for vv in range(2):
                        col = slice((2 * u + vv) * P, (2 * u + vv + 1) * P)
                        ins = product(w[:, vv * S:(vv + 1) * S],
                                      [(cut(W0["k"], every, c, col), cut(T2, every, c, every)) for c in range(C)])
                    filled(ins, f"k{u}")
                for u in range(4):
                    w = wait_work_free(pe, i, f"v{u}")
                    kh, half = u // 2, u % 2
                    filled(product(w[:, :], [(cut(T2, every, c, slice(kh * P, (kh + 1) * P)),
                                              cut(W0["v"], every, c, slice(512 * half, 512 * half + 512)))
                                             for c in range(C)]), f"v{u}")
                wait_split("q3")
                wait_split("k3")
                wait_split("v3")

                def score(p):
                    for a in range(2):
                        pe.wait_ge(a_free[a], A_USES * i + p)
                        for qh in range(2):
                            ins = t.matmul(A[a][:, qh * S:(qh + 1) * S], QZ0[:, a, p, qh * P:(qh + 1) * P],
                                           KT0[:, p, :], start=True, stop=True)
                        ins.then_inc(a_full[a], 1)

                def turn(p):
                    if p >= 2:
                        pe.wait_ge(exp_done, 3 * NP * i + p - 1)
                    else:
                        pe.wait_ge(exp_done, 3 * NP * i)
                    for a in range(2):
                        pe.wait_ge(shifted, H * i + 2 * p + a + 1)
                        for kh in range(2):
                            for qh in range(2):
                                ins = t.transpose(SC[p % 2][:, a, kh, qh * P:(qh + 1) * P],
                                                  ring[:, p % NR, a, qh, kh * P:(kh + 1) * P], ident[:, :])
                    ins.then_inc(sc_full, 1)

                def weigh(p):
                    pe.wait_ge(exp_done, 3 * NP * i + p + 1)
                    w = wait_work_free(pe, i, f"pv{p}")
                    for a in range(2):
                        for qh in range(2):
                            at = (2 * a + qh) * DV
                            for kh in range(2):
                                ins = t.matmul(w[:, at:at + DV], PT[:, p % 2, a, kh, qh * P:(qh + 1) * P],
                                               V0[:, kh, 2 * p + a, :], start=kh == 0, stop=kh == 1)
                                if a == 0 and qh == 0 and kh == 0:
                                    ins.then_inc(ring_free, 1)
                    filled(ins, f"pv{p}")

                for p in range(NP + 2):
                    if p < NP:
                        score(p)
                    if p >= 2:
                        weigh(p - 2)
                    if 1 <= p <= NP:
                        turn(p - 1)

                wait_split("pv7")

                def ct(u):
                    w = wait_work_free(pe, i, f"ct{u}")
                    for c in range(2):
                        for h in range(2):
                            ins = t.transpose(w[:, c * S + h * P:c * S + (h + 1) * P],
                                              ctx_cat[:, h, (2 * u + c) * P:(2 * u + c + 1) * P], ident[:, :])
                    filled(ins, f"ct{u}")

                def project(u):
                    wait_split(f"ct{u}")
                    T = (T1, T2)[u % 2]
                    for h in range(2):
                        if u == 0:
                            pe.wait_ge(a_free[h], A_USES * i + NP)
                        for c in range(2):
                            terms = [(T[x][:, c, h * P:(h + 1) * P], Wo[y][:, 2 * u + c, :])
                                     for x, y in ((0, 0), (0, 1), (1, 0))]
                            for k, (a, b) in enumerate(terms):
                                ins = t.matmul(A[h][:, 0:D], a, b, start=u == 0 and c == 0 and k == 0,
                                               stop=u == 3 and c == 1 and k == 2)
                        if u == 3:
                            ins.then_inc(a_full[h], 1)

                for u in range(5):
                    if u < 4:
                        ct(u)
                    if u >= 1:
                        project(u - 1)

                def decoder(m):
                    tg = "ab"[m]
                    causal = m == 0
                    pe.wait_ge(norm_done, 4 * i + m + 1)
                    transpose4(f"{tg}.T", cur)
                    kv = T1
                    wq, wk, wv = (W1[f"{n}{m + 1}"] for n in "qkv")
                    if m == 1:
                        pe.wait_ge(cm_ready, i + 1)
                        transpose4("b.cT", c_nat)
                        kv = T2
                    wait_split(f"{tg}.T")
                    for name, w_, T in ((f"{tg}.q", wq, T1), (f"{tg}.k", wk, kv)):
                        if name == "b.k":
                            wait_split("b.cT")
                        w = wait_work_free(pe, i, name)
                        for gr in range(2):
                            ins = product(w[:, gr * S:(gr + 1) * S],
                                          [(cut(w_, every, c, slice(gr * P, (gr + 1) * P)), cut(T, every, c, every))
                                           for c in range(C)])
                            if m == 1 and gr == 0 and name == "b.q":
                                ins.then_inc(c_used, 1)
                        filled(ins, name)
                    pe.wait_ge(q0blk_ready, 2 * i + m + 1)
                    wait_read(pe, i, f"{tg}.k")
                    w = wait_work_free(pe, i, f"{tg}.e0")
                    for gr in range(2):
                        ins = t.matmul(w[:, gr * S:(gr + 1) * S], Q0blk[:, gr], K1[:, gr], start=True, stop=True)
                    filled(ins, f"{tg}.e0")
                    pe.wait_ge(sel_ready, 2 * i + m + 1)
                    w = wait_work_free(pe, i, f"{tg}.len")
                    filled(t.matmul(w[:, 0:H], ones[:, :], sel_len[:, :], start=True, stop=True), f"{tg}.len")
                    w = wait_work_free(pe, i, f"{tg}.v")
                    for kh in range(2):
                        ins = product(w[:, kh * D:(kh + 1) * D],
                                      [(cut(kv, every, c, slice(kh * P, (kh + 1) * P)), cut(wv, every, c, every))
                                       for c in range(C)])
                    filled(ins, f"{tg}.v")

                    def rows_of(gr):
                        return slice(64 * gr, 64 * gr + SPLIT + 1)

                    pe.wait_ge(stacks_in, 16 * 14 * (2 * i + m + 1))
                    for p in range(NP):
                        for gr in range(2):
                            pe.wait_ge(a_free[gr], A_USES * i + NP + 1 + NP * m + p)
                            for qh in range(2):
                                ins = t.matmul(A[gr][:, qh * S:(qh + 1) * S], QS1[rows_of(gr), p, qh * P:(qh + 1) * P],
                                               KS1[rows_of(gr), p, :], start=True, stop=not causal)
                                if causal:
                                    lo = qh * P
                                    ins = t.matmul(A[gr][:, qh * S + lo:(qh + 1) * S], identb[:, :],
                                                   mask_q[:, 0:S - lo], start=False, stop=True)
                            ins.then_inc(a_full[gr], 1)
                    for gr in range(2):
                        pe.wait_ge(a_free[gr], A_USES * i + NP + 1 + NP * (m + 1))
                    w = wait_work_free(pe, i, f"{tg}.mT")
                    for qh in range(2):
                        ins = t.transpose(w[0:H, qh * P:(qh + 1) * P], neg_max[:, qh, :], ident[:, :])
                    filled(ins, f"{tg}.mT")

                    def turn(p):
                        if p >= 2:
                            pe.wait_ge(exp_done, 3 * NP * i + NP * (1 + m) + p - 1)
                        else:
                            pe.wait_ge(exp_done, 3 * NP * i + NP * (1 + m))
                        for gr in range(2):
                            for kh in range(2):
                                dst = SC[p % 2][:, gr, kh, :]
                                ins = t.matmul(dst, KS1[rows_of(gr), p, kh * P:(kh + 1) * P], QS1[rows_of(gr), p, :],
                                               start=True, stop=not causal)
                                if causal:
                                    ins = t.matmul(SC[p % 2][:, gr, kh, 0:(kh + 1) * P], identb[:, :],
                                                   mask_k[:, (1 - kh) * P:2 * P], start=False, stop=True)
                        ins.then_inc(sc_full, 1)

                    def weigh(p):
                        pe.wait_ge(exp_done, 3 * NP * i + NP * (1 + m) + p + 1)
                        u = p // 2
                        name = f"{tg}.pv{u // 2}"
                        if p % 4 == 0:
                            wait_work_free(pe, i, name)
                        w = W[work(name)[0]]
                        for gr in range(2):
                            r = 32 * (2 * (p % 2) + gr)
                            for kh in range(2):
                                lo = P if causal and kh == 1 else 0
                                ins = t.matmul(w[r:r + 32, (u % 2) * S + lo:(u % 2 + 1) * S],
                                               V1[:, kh, NP * gr + p, :], PT[:, p % 2, gr, kh, lo:S],
                                               start=kh == 0, stop=kh == 1, tile_position=(0, r))
                        if p % 4 == 3:
                            filled(ins, name)
                        else:
                            ins.then_inc(pv_done, 1)

                    pe.wait_ge(max_in, 32 * (2 * i + m + 1))
                    pe.wait_ge(v1_ready, 2 * i + m + 1)
                    for p in range(NP + 1):
                        if p < NP:
                            turn(p)
                        if p >= 1:
                            weigh(p - 1)
                    wait_read(pe, i, f"{tg}.pv0")
                    wait_read(pe, i, f"{tg}.pv1")
                    for h in range(2):
                        w = wait_work_free(pe, i, f"{tg}.z{h}")
                        for u in range(4):
                            ins = t.transpose(w[:, u * P:(u + 1) * P], z_raw[:, u, h * P:(h + 1) * P], ident[:, :])
                        filled(ins, f"{tg}.z{h}")

                decoder(0)
                decoder(1)
                pe.wait_ge(norm_done, 4 * i + 3)
                transpose4("f.T", cur)
                wait_split("f.T")
                w = wait_work_free(pe, i, "f.h")
                for c2 in range(C):
                    ins = product(w[:, c2 * S:(c2 + 1) * S],
                                  [(cut(W1["f1"], every, c, slice(c2 * P, (c2 + 1) * P)), cut(T1, every, c, every))
                                   for c in range(C)])
                filled(ins, "f.h")
                wait_split("f.h")
                w = wait_work_free(pe, i, "f.o")
                for h in range(2):
                    ins = product(w[:, h * D:(h + 1) * D],
                                  [(cut(T2, every, c, slice(h * P, (h + 1) * P)), cut(W1["f2"], every, c, every))
                                   for c in range(C)])
                filled(ins, "f.o")


def kernel(x, ctx_1024, fside_Bx16xSxS2_0, **v):
    import concourse.bacc as bacc
    from concourse.bass_utils import run_bass_kernel_spmd

    a0 = {k[len("L0_xattn_"):]: a for k, a in v.items() if k.startswith("L0_")}
    a1 = {k[len("L1_xattn_"):]: a for k, a in v.items() if k.startswith("L1_")}
    D = x.shape[-1]

    def heads_as_columns(w):
        return np.asarray(w).transpose(1, 0, 2).reshape(D, -1)

    arrays = {"x": x, "ctx": ctx_1024, "fside": fside_Bx16xSxS2_0}
    for n in "qkvo":
        arrays["w0" + n] = a0["w" + n]
    for n in ("q", "k", "v"):
        for layer in "12":
            arrays[f"w1{n}{layer}"] = heads_as_columns(a1[f"W{n}{layer}"])
    arrays["w1f1"] = np.asarray(a1["fc1_w"]).T
    arrays["w1f2"] = np.asarray(a1["fc2_w"]).T
    for n, a in (("bq", a0["bq"]), ("bk", a0["bk"]), ("bv", a0["bv"]), ("fb", a1["fc1_b"])):
        arrays["vec0" + n] = a
    for n, a in (("bo", a0["bo"]), ("ln_g", a0["ln_g"]), ("ln_b", a0["ln_b"]), ("fc2_b", a1["fc2_b"]),
                 ("ln1_g", a1["ln1_g"]), ("ln1_b", a1["ln1_b"]), ("ln2_g", a1["ln2_g"]), ("ln2_b", a1["ln2_b"]),
                 ("ln3_g", a1["ln3_g"]), ("ln3_b", a1["ln3_b"])):
        arrays["vec1" + n] = a
    arrays = {n: np.ascontiguousarray(a) for n, a in arrays.items()}

    nc = bacc.Bacc("TRN2", target_bir_lowering=False, num_devices=1)
    dram = {n: nc.dram_tensor("in_" + n, a.shape, mybir.dt.from_np(a.dtype), kind="ExternalInput").ap()
            for n, a in arrays.items()}

    def group(prefix):
        return {n[len(prefix):]: ap for n, ap in dram.items() if n.startswith(prefix)}

    out = nc.dram_tensor("out", x.shape, F32, kind="ExternalOutput").ap()
    build(nc, dram["x"], dram["ctx"], dram["fside"], group("w0"), group("vec0"), group("w1"), group("vec1"), out)
    r = run_bass_kernel_spmd(nc, [{"in_" + n: a for n, a in arrays.items()}], core_ids=[0])
    return r.results[0]["out"]
```

```python
from contextlib import ExitStack

import numpy as np

import concourse.bass as bass
from concourse import mybir

P = 128
F32 = mybir.dt.float32
F32R = mybir.dt.float32r
BF16 = mybir.dt.bfloat16
I32 = mybir.dt.int32
ALU = mybir.AluOpType
ACT = mybir.ActivationFunctionType
AX = mybir.AxisListType

BIG = 1.0e30
LN_EPS0 = 1e-6
LN_EPS1 = 1e-5
X_STEPS, Y_STEPS = 20, 51

SCHEDULE = """
x.in a.T x.v0 x.v1 a.q a.k a.first x.v2 x.v3 x.qk0 x.qk1 x.sc0 x.qk2 a.v a.len x.tn0 x.sc1 x.wg0 x.qk3 x.tn1
a.A0 x.wg1 a.A1 x.sc2 a.A2 a.A3 x.tn2 a.A4 a.A5 x.wg2 a.A6 a.A7 a.mT x.sc3 x.qk4 x.tn3 a.Bt0 x.sc4 x.wg3
a.Bt1 a.Bw0 a.Bt2 a.Bw1 a.Bt3 a.Bw2 a.Bt4 a.Bw3 a.Bt5 x.qk5 a.Bw4 a.Bt6 a.Bw5 a.Bw6 a.Bt7 x.tn4 a.Bw7 a.z
x.qk6 x.sc5 b.T x.wg4 x.tn5 b.cT b.q b.k b.first x.wg5 x.sc6 b.v b.len x.qk7 x.tn6 x.sc7 x.wg6 x.tn7 b.A0
b.A1 b.A2 b.A3 b.A4 x.wg7 b.A5 x.ct0 x.ct1 b.A6 b.A7 b.mT x.keep x.pr0 x.ct2 x.pr1 x.ct3 x.pr2 b.Bt0 b.Bt1
b.Bw0 b.Bt2 x.pr3 b.Bw1 b.Bt3 b.Bw2 b.Bt4 b.Bw3 b.Bt5 b.Bw4 b.Bw5 b.Bt6 b.Bt7 b.Bw6 x.ln b.Bw7 b.z f.T f.h
f.o
""".split()


class Body:

    def __init__(self, i, batches):
        self.i = i
        peeled = isinstance(i, int)
        self.peeled = peeled
        self.order = [s for s in SCHEDULE if not (peeled and i == (batches if s[0] == "x" else 0))]
        self.work, self.scores, self.pairs, self.norms = map(self.uses, (WORK, SCORES, PAIRS, NORMS))
        self.steps = 0

    def uses(self, kinds):
        return {n: k for k, n in enumerate(n for s in self.order for n in uses_of(s, kinds))}

    def count(self, kinds, place, per=1):
        return self.total(len(totals(kinds, "x")) // per, len(totals(kinds, "y")) // per, place // per)

    def total(self, in_x, in_y, here):
        if self.peeled and self.i == 0:
            return here
        return (in_x + in_y) * self.i + (here - in_y)


def step_name(s):
    part, rest = s.split(".")
    kind = rest.rstrip("0123456789")
    return part, (kind if part in "ab" else f"{part}.{kind}"), rest[len(kind):]


WORK = {"x.in": ("xT", "cT"), "x.v": "0123", "x.qk": "01234567", "x.wg": "01234567", "x.ct": "0123",
        "T": "", "cT": "", "q": "", "k": "", "first": "", "v": "", "len": "", "mT": "", "Bw": "0246",
        "z": ("z0", "z1"), "f.T": "", "f.h": "", "f.o": ""}
SCORES = {"x.sc": "01234567", "x.pr": "0", "A": "01234567"}
PAIRS = {"x.tn": "01234567", "Bt": "01234567"}
NORMS = {"x.ln": "", "z": "", "f.o": ""}


def uses_of(s, kinds):
    part, name, number = step_name(s)
    if name not in kinds:
        return []
    if isinstance(kinds[name], tuple):
        return [f"{part}.{use}" for use in kinds[name]]
    return [s] if number in kinds[name] else []


def totals(kinds, part):
    return [n for s in SCHEDULE if (s[0] == "x") == (part == "x") for n in uses_of(s, kinds)]


def check_schedule():
    for order in (SCHEDULE, [s for s in SCHEDULE if s[0] == "x"], [s for s in SCHEDULE if s[0] != "x"]):
        at = {s: k for k, s in enumerate(order)}
        turns = [s for s in order if uses_of(s, PAIRS)]
        weighs = [s.replace("tn", "wg").replace("Bt", "Bw") for s in turns]
        for n in range(len(turns)):
            assert at[turns[n]] < at[weighs[n]], turns[n]
            assert n < 2 or at[weighs[n - 2]] < at[turns[n]], turns[n]
            assert n + 1 == len(turns) or turns[n][0] != turns[n + 1][0] or at[weighs[n]] < at[weighs[n + 1]]
        if "x.in" in at:
            for p in range(8):
                assert at[f"x.qk{p}"] < at[f"x.sc{p}"] < at[f"x.tn{p}"]
                assert p < 2 or at[f"x.sc{p - 2}"] < at[f"x.qk{p}"]
            assert at["x.in"] == min(k for s, k in at.items() if s[0] == "x")
            assert max(at[f"x.v{u}"] for u in range(4)) < at["x.wg0"]
            assert max(at["x.wg7"], at["x.qk7"]) < at["x.ct0"] and at["x.pr3"] < at["x.ln"]
            for u in range(4):
                assert at[f"x.ct{u}"] < at[f"x.pr{u}"] and (u < 2 or at[f"x.pr{u - 2}"] < at[f"x.ct{u}"])
                assert u == 0 or at[f"x.ct{u - 1}"] < at[f"x.ct{u}"] and at[f"x.pr{u - 1}"] < at[f"x.pr{u}"]
            between = order[at["x.pr0"]:at["x.ln"]]
            assert not [s for s in between[1:] if uses_of(s, SCORES)]
        if "a.z" in at and "x.in" in at:
            assert at["a.z"] < at["x.ln"] and at["b.cT"] < at["x.keep"]
        for part in "ab":
            for p in (0, 2, 4, 6):
                if "a.z" in at:
                    between = order[at[f"{part}.Bw{p}"] + 1:at[f"{part}.Bw{p + 1}"]]
                    assert sum(len(uses_of(s, WORK)) for s in between) <= 1, (part, p)
    for kinds in (WORK, PAIRS):
        assert len(totals(kinds, "x")) % 2 == 0 and len(totals(kinds, "y")) % 2 == 0


def build(nc, x, ctx_in, fside, w0, vec0, w1, vec1, out):
    B, S, D = x.shape
    H = fside.shape[1]
    DK0 = 64
    DK1 = D // H
    C = D // P
    NP = H // 2
    E0 = H * DK0
    DV = DK0 + 1
    SPLIT = 3 * DK1
    assert S == 2 * P and C == 2 and H == 16 and DK1 == 16
    check_schedule()

    stack = ExitStack()
    with stack:
        def sb(name, shape, dt=F32):
            return stack.enter_context(nc.sbuf_tensor(name, shape, dt))

        def sem(name):
            return stack.enter_context(nc.semaphore(name))

        W0 = {n: [sb(f"w0{n}_{p}", [P, C, E0], F32R) for p in ("hi", "lo")] for n in "qkv"}
        Wo = [sb(f"w0o_{p}", [P, E0 // P, D], F32R) for p in ("hi", "lo")]
        W1 = {n: [sb(f"w1{n}_{p}", [P, C, D], F32R) for p in ("hi", "lo")] for n in w1}
        bv_col = sb("bv_col", [P, E0 // P])
        bv_parts = [sb(f"bv_{p}", [P, E0 // P], F32R) for p in ("hi", "lo")]
        rows = sb("rows", [P, len(vec1), D])
        row = {n: rows[:, k, :] for k, n in enumerate(vec1)}
        bq_col = sb("bq_col", [P, NP])
        bk_col = sb("bk_col", [P, NP])
        fb_col = sb("fb_col", [P, C])
        ident = sb("ident", [P, P])
        identb = sb("identb", [P, P], BF16)
        ones = sb("ones", [P, P])
        mask_q = sb("mask_q", [P, 2 * P], BF16)
        mask_k = sb("mask_k", [P, 2 * P], BF16)
        blk = sb("blk", [P, P])
        sel = sb("sel", [P, P // DK1])
        key_row = sb("key_row", [P, S])
        key_col = sb("key_col", [P, 2])
        neg_half = sb("neg_half", [P, 2])
        c_load = sb("c_load", [P, 2, D])
        x_nat = sb("x_nat", [P, 2, D])
        T1x = [sb(f"T1x_{p}", [P, C, S], F32R) for p in ("hi", "lo")]
        T2x = [sb(f"T2x_{p}", [P, C, S], F32R) for p in ("hi", "lo")]
        QZ0 = sb("QZ0", [P, 2, 2, S])
        KT0 = sb("KT0", [P, 2, S])
        V0 = sb("V0", [P, 2, H, DV])
        NR = 2
        ring = sb("ring", [P, NR, 2, 2, S])
        low = sb("low", [P, NR, 2, 2])
        PT = sb("PT", [P, 2, 2, 2, S])
        ctx_cat = sb("ctx_cat", [P, 2, E0])
        rec0 = sb("rec0", [P, 2, 2])
        x1 = sb("x1", [P, 2, D])
        c_keep = sb("c_keep", [P, 2, D])
        T1 = [sb(f"T1_{p}", [P, C, S], F32R) for p in ("hi", "lo")]
        T2 = [sb(f"T2_{p}", [P, C, S], F32R) for p in ("hi", "lo")]
        cur = sb("cur", [P, 2, D])
        tmp = sb("tmp", [P, 2, D])
        result = sb("result", [P, 2, D])
        stage = sb("stage", [P, 2048])
        parts = stage[:, :].rearrange("p (w s g t) -> p w s g t", w=2, s=2, g=2)
        V1 = stage[:, 0:4 * S].rearrange("p (k h e) -> p k h e", k=2, h=H)
        z_raw = stage[:, 4 * S:8 * S].rearrange("p (u t) -> p u t", u=4)
        K1 = sb("K1", [P, 2, S])
        QS1 = sb("QS1", [P, NP, S], F32R)
        KS1 = sb("KS1", [P, NP, S], F32R)
        q0c = sb("q0c", [P, 2])
        k0c = sb("k0c", [P, 2])
        junk = tmp[:, 0, :]
        Q0blk = tmp[:, 1, :].rearrange("p (g c) -> p g c", g=2)
        drop = tmp[:, :, :].bitcast(I32)
        max_row = tmp[0:H, 0, :].bitcast(F32R)
        length = sb("length", [P, 2])
        sel_len = sb("sel_len", [P, H])
        keep = sb("keep", [P, 2, H])
        neg_max = sb("neg_max", [P, 2, H])
        mask0 = sb("mask0", [P, 2])
        mask1 = sb("mask1", [P, 2])
        rec1 = sb("rec1", [P, H])
        st = sb("st", [P, 2, 6])
        mv = sb("mv", [P, 2, 2])
        veps = sb("veps", [P, 2])
        rstd = sb("rstd", [P, 2])
        carrier = sb("carrier", [P, 64])

        A = [stack.enter_context(nc.psum_tensor(f"A{n}", [P, 512], F32)) for n in range(2)]
        SC = [stack.enter_context(nc.psum_tensor(f"SC{n}", [P, 2, 2, S], F32)) for n in range(2)]
        W = [stack.enter_context(nc.psum_tensor(f"W{n}", [P, 512], F32)) for n in range(2)]

        weights_in = [sem(f"weights_in{n}") for n in range(2)]
        weights1_in = sem("weights1_in")
        vectors_in = sem("vectors_in")
        hi_ready = sem("hi_ready")
        bv_step = sem("bv_step")
        bvo_full = sem("bvo_full")
        bo_ready = sem("bo_ready")
        split_ready = sem("split_ready")
        consts_ready = sem("consts_ready")
        pool_step = sem("pool_step")
        x_in = sem("x_in")
        c_in = sem("c_in")
        bias_in = [sem(f"bias_in{n}") for n in range(NR)]
        xb_ready = sem("xb_ready")
        work_full = [sem(f"work_full{n}") for n in range(2)]
        work_free = [sem(f"work_free{n}") for n in range(2)]
        a_full = [sem(f"a_full{n}") for n in range(2)]
        a_free = [sem(f"a_free{n}") for n in range(2)]
        shifted = sem("shifted")
        sc_full = sem("sc_full")
        exp_done = sem("exp_done")
        stats_ready = sem("stats_ready")
        veps_ready = sem("veps_ready")
        rstd_ready = sem("rstd_ready")
        x_norm = sem("x_norm")
        y_norm = sem("y_norm")
        kept = sem("kept")
        cm_ready = sem("cm_ready")
        q0_ready = sem("q0_ready")
        q0blk_ready = sem("q0blk_ready")
        sel_ready = sem("sel_ready")
        k1_ready = sem("k1_ready")
        qhi_ready = sem("qhi_ready")
        khi_ready = sem("khi_ready")
        k_parts = sem("k_parts")
        q_stored = sem("q_stored")
        k_stored = sem("k_stored")
        stacks_in = sem("stacks_in")
        v1_ready = sem("v1_ready")
        max_out = sem("max_out")
        max_in = sem("max_in")
        out_stored = sem("out_stored")
        dve_step = sem("dve_step")

        STACK_LOADS = 12
        scratch = nc.dram_tensor("scratch", [2, 2, 2, P, S], F32).ap()

        max_scratch = nc.dram_tensor("max_scratch", [H, S], F32).ap()

        SCALE0 = 0.5 / float(DK0) ** 0.5
        SCALE1 = 1.0 / float(DK1) ** 0.5

        def wait_at_least(eng, signal, value):
            if not isinstance(value, int) or value > 0:
                eng.wait_ge(signal, value)

        def bank(b, name):
            return b.work[name] % 2

        def wait_read(eng, b, *names, before=None):
            for n in range(2):
                places = [b.work[m] + 2 for m in names] + ([b.work[before]] if before else [])
                places = [k for k in places if k % 2 == n]
                if places:
                    wait_at_least(eng, work_free[n], b.count(WORK, max(places), 2))

        def wait_work_free(eng, b, name, read=()):
            wait_read(eng, b, *read, before=name)
            return W[bank(b, name)]

        def wait_work_full(eng, b, name):
            eng.wait_ge(work_full[bank(b, name)], b.count(WORK, b.work[name] + 2, 2))
            return W[bank(b, name)]

        def layer_number(b, m):
            return 2 * b.i + (m - 2)

        carriers = []

        def part_wait(eng, b):
            if b.peeled:
                return
            column = carrier[:, len(carriers):len(carriers) + 1]
            carriers.append(column)
            if eng.engine == nc.vector.engine:
                nc.vector.memset(column, 0.0)
            else:
                nc.gpsimd.tensor_tensor(column, neg_half[:, 0:1], neg_half[:, 0:1], ALU.add)

        def filled(ins, b, name):
            return ins.then_inc(work_full[bank(b, name)], 1)

        def freed(ins, b, name):
            return ins.then_inc(work_free[bank(b, name)], 1)

        def run(b, steps):
            for s in b.order:
                part, name, k = step_name(s)
                if name in steps:
                    steps[name](*([] if part in "xf" else ["ab".index(part)]), *([int(k)] if k else []))

        bv_wide = [T[:, 0:4, :].rearrange("p j (e c) -> p (j e) c", e=2) for T in (QS1, KS1)]
        weight_list = [(w0[n], W0[n]) for n in "qkv"] + [(w0["o"], Wo)]
        staged = [stage[:, :], ctx_cat[:, :, :].rearrange("p h e -> p (h e)")]
        weight_list1 = [(w1[n], W1[n]) for n in w1]
        staged1 = [stage[:, k * C * D:(k + 1) * C * D] for k in range(4)] + [
            t[:, :, :].rearrange("p c n -> p (c n)") for t in (cur, tmp, result, K1)]

        block = stack.enter_context(nc.Block())

        @block.sync
        def _(sp):
            for n, (dram, _) in enumerate(weight_list):
                if n >= 2:
                    sp.wait_ge(split_ready, n - 1)
                sp.dma_start(staged[n % 2].rearrange("p (c n) -> p c n", n=dram.shape[1]),
                             dram.rearrange("(c p) n -> p c n", p=P)).then_inc(weights_in[n % 2], 16)
                if n == 0:
                    nvec = 0
                    for dst_v, src_v in [(bv_col[:, :], vec0["bv"].rearrange("(j r) -> r j", r=P)),
                                         (bq_col[:, :], vec0["bq"].rearrange("(j r) -> r j", r=P)),
                                         (bk_col[:, :], vec0["bk"].rearrange("(j r) -> r j", r=P)),
                                         (fb_col[:, :], vec0["fb"].rearrange("(j r) -> r j", r=P))] + [
                                             (row[m], vec1[m].partition_broadcast(P)) for m in vec1]:
                        sp.dma_start(dst_v, src_v, allow_slow_non_contiguous=True).then_inc(vectors_in, 16)
                        nvec += 1

            def body(i):
                b = Body(i, B)

                def bias(p):
                    sp.dma_start(ring[:, p % NR], fside[i, 2 * p:2 * p + 2].rearrange("a (h q) k -> q a h k", q=P))\
                        .then_inc(bias_in[p % NR], 16)

                def load():
                    wait_at_least(sp, sc_full, b.count(PAIRS, 0))
                    wait_at_least(sp, x_norm, i)
                    sp.dma_start(x_nat[:, :, :], x[i].rearrange("(h p) d -> p h d", p=P)).then_inc(x_in, 16)
                    wait_at_least(sp, kept, i)
                    sp.dma_start(c_load[:, :, :], ctx_in[i].rearrange("(h p) d -> p h d", p=P)).then_inc(c_in, 16)
                    for p in range(NR):
                        bias(p)

                def turn_x(p):
                    if p + NR < NP:
                        sp.wait_ge(sc_full, b.count(PAIRS, b.pairs[f"x.tn{p}"]) + 1)
                        bias(p + NR)

                def queries(m):
                    wait_read(sp, b, f"{'ab'[m]}.q")
                    sp.dma_start(scratch[0].rearrange("s g p t -> p s g t"), parts[:, 0]).then_inc(q_stored, 16)

                def query_stacks(m):
                    sp.wait_ge(q_stored, 16 * layer_number(b, m) + 16)
                    for gr in range(2):
                        for c, part in enumerate((0, 1, 0)):
                            sp.dma_start(QS1[64 * gr + DK1 * c:64 * gr + DK1 * (c + 1)].bitcast(F32),
                                         scratch[0, part, gr].rearrange("(j d) t -> d j t", d=DK1))\
                                .then_inc(stacks_in, 16)

                def keys(m):
                    sp.wait_ge(k_parts, layer_number(b, m) + 1)
                    sp.dma_start(scratch[1].rearrange("s g p t -> p s g t"), parts[:, 1]).then_inc(k_stored, 16)
                    sp.wait_ge(k_stored, 16 * layer_number(b, m) + 16)
                    for gr in range(2):
                        for c, part in enumerate((0, 0, 1)):
                            sp.dma_start(KS1[64 * gr + DK1 * c:64 * gr + DK1 * (c + 1)].bitcast(F32),
                                         scratch[1, part, gr].rearrange("(j d) t -> d j t", d=DK1))\
                                .then_inc(stacks_in, 16)

                def maxima(m):
                    wait_read(sp, b, f"{'ab'[m]}.mT")
                    sp.dma_start(max_scratch, max_row.bitcast(F32)).then_inc(max_out, 16)
                    sp.wait_ge(max_out, 16 * layer_number(b, m) + 16)
                    for gr in range(2):
                        sp.dma_start(QS1[64 * gr + SPLIT:64 * gr + SPLIT + 1].bitcast(F32),
                                     max_scratch[NP * gr:NP * (gr + 1), :].unsqueeze(0)).then_inc(max_in, 16)

                run(b, {"x.in": load, "x.tn": turn_x, "q": queries, "k": query_stacks, "len": keys, "mT": maxima})

            body(0)
            sp.wait_ge(split_ready, len(weight_list))
            for (dram, _), dst in zip(weight_list1, staged1):
                sp.dma_start(dst.rearrange("p (c n) -> p c n", c=C),
                             dram.rearrange("(c p) n -> p c n", p=P)).then_inc(weights1_in, 16)
            with sp.Fori(1, B) as i:
                body(i)
            body(B)

        @block.gpsimd
        def _(pool):
            g = nc.gpsimd
            n = [0]

            def step(ins):
                n[0] += 1
                ins.then_inc(pool_step, 1)
                pool.wait_ge(pool_step, n[0])

            step(g.memset(ones[:, :], 1.0))
            step(g.memset(ident[:, :], 0.0))
            step(g.affine_select(out=ident[:, :], in_=ident[:, :], compare_op=ALU.not_equal, fill=1.0,
                                 base=0, pattern=[[-1, P]], channel_multiplier=1))
            step(g.tensor_copy(identb[:, :], ident[:, :]))
            step(g.memset(mask_q[:, :], -BIG))
            step(g.memset(mask_k[:, :], -BIG))
            step(g.affine_select(out=mask_q[:, 0:P], in_=mask_q[:, 0:P], compare_op=ALU.is_gt, fill=0.0,
                                 base=0, pattern=[[1, P]], channel_multiplier=-1))
            step(g.affine_select(out=mask_k[:, P:2 * P], in_=mask_k[:, P:2 * P], compare_op=ALU.is_gt, fill=0.0,
                                 base=0, pattern=[[-1, P]], channel_multiplier=1))
            for t, inner in ((blk, [[0, DK1]]), (sel, [])):
                v = t[:, :].rearrange("p (j d) -> p j d", d=DK1) if inner else t[:, :]
                step(g.memset(t[:, :], 1.0 if inner else 1.0 / DK1))
                step(g.affine_select(out=v, in_=v, compare_op=ALU.is_ge, fill=0.0, base=0,
                                     pattern=[[-DK1, P // DK1]] + inner, channel_multiplier=1))
                step(g.affine_select(out=v, in_=v, compare_op=ALU.is_ge, fill=0.0, base=DK1 - 1,
                                     pattern=[[DK1, P // DK1]] + inner, channel_multiplier=-1))
            step(g.iota(drop[:, 0], [[1, S]], base=0, channel_multiplier=0))
            step(g.tensor_copy(key_row[:, :], drop[:, 0]))
            step(g.iota(drop[:, 0, 0:2], [[P, 2]], base=0, channel_multiplier=1))
            step(g.tensor_copy(key_col[:, :], drop[:, 0, 0:2]))
            step(g.memset(QZ0[:, :, :, :], 0.0))
            step(g.memset(V0[:, :, :, DK0:DV], 1.0))
            step(g.memset(neg_half[:, :], -0.5))
            pool.wait_ge(vectors_in, 16 * (4 + len(vec1)))
            g.tensor_scalar(bq_col[:, :], bq_col[:, :], SCALE0, 1.0, ALU.mult, ALU.mult).then_inc(consts_ready, 1)

            pool.wait_ge(bo_ready, 1)
            step(g.memset(KS1[:, :, :].bitcast(F32), 1.0))

            def body(i):
                b = Body(i, B)

                def residual():
                    wait_work_full(pool, b, "x.xT")
                    for h in range(2):
                        ins = g.tensor_tensor(x_nat[:, h], x_nat[:, h], row["bo"], ALU.add)
                    ins.then_inc(xb_ready, 1)

                def shift(p):
                    for a in range(2):
                        pool.wait_ge(a_free[a], b.count(SCORES, b.scores[f"x.sc{p}"]) + 1)
                        part_wait(pool, b)
                        for qh in range(2):
                            s = ring[:, p % NR, a, qh]
                            ins = g.tensor_scalar(s, s, -1.0, low[:, p % NR, a, qh:qh + 1], ALU.mult, ALU.add)
                        ins.then_inc(shifted, 1)

                def keep_context():
                    pool.wait_ge(c_in, 16 * i + 16)
                    if "b.cT" in b.work:
                        wait_work_full(pool, b, "b.cT")
                        part_wait(pool, b)
                    for h in range(2):
                        ins = g.tensor_copy(c_keep[:, h], c_load[:, h])
                    ins.then_inc(kept, 1)

                def power(name, eps):
                    n = b.count(NORMS, b.norms[name]) + 1
                    pool.wait_ge(stats_ready, n)
                    part_wait(pool, b)
                    g.tensor_scalar(veps[:, :], mv[:, :, 1], eps, 1.0, ALU.add, ALU.mult).then_inc(veps_ready, 1)
                    pool.wait_ge(veps_ready, n)
                    g.tensor_tensor(rstd[:, :], veps[:, :], neg_half[:, :], ALU.pow).then_inc(rstd_ready, 1)

                def first_query(m):
                    pool.wait_ge(q0_ready, layer_number(b, m) + 1)
                    part_wait(pool, b)
                    for gr in range(2):
                        ins = g.tensor_scalar(Q0blk[:, gr], blk[:, :], q0c[:, gr:gr + 1], 1.0, ALU.mult, ALU.mult)
                    ins.then_inc(q0blk_ready, 1)

                def output():
                    power("f.o", LN_EPS1)
                    pool.wait_ge(y_norm, 3 * i)
                    pool.dma_start(out[i - 1].rearrange("(h p) d -> p h d", p=P), result[:, :, :]).then_inc(out_stored, 16)
                    pool.wait_ge(out_stored, 16 * i)

                run(b, {"x.in": residual, "x.sc": shift, "x.keep": keep_context,
                        "x.ln": lambda: power("x.ln", LN_EPS0), "q": first_query,
                        "z": lambda m: power(f"{'ab'[m]}.z", LN_EPS1), "f.o": output})

            body(0)
            with pool.Fori(1, B) as i:
                body(i)
            body(B)

        @block.scalar
        def _(act):
            s = nc.scalar
            for n, (_, (hi, lo)) in enumerate(weight_list):
                act.wait_ge(weights_in[n % 2], 16 * (n // 2 + 1))
                s.activation(hi[:, :, :].rearrange("p c n -> p (c n)"), staged[n % 2], ACT.Copy).then_inc(hi_ready, 1)
            act.wait_ge(consts_ready, 1)

            def body(i):
                b = Body(i, B)

                def queries_keys_x(p):
                    w = wait_work_full(act, b, f"x.qk{p}")
                    for a in range(2):
                        r = slice(64 * a, 64 * a + 64)
                        s.activation(QZ0[r, a, p % 2], w[r, 0:S], ACT.Identity, bias=bq_col[r, p:p + 1], scale=SCALE0)
                    freed(s.activation(KT0[:, p % 2], w[:, S:2 * S], ACT.Identity, bias=bk_col[:, p:p + 1]),
                          b, f"x.qk{p}")

                def values_x(u):
                    w = wait_work_full(act, b, f"x.v{u}")
                    freed(s.activation(V0[:, u // 2, 8 * (u % 2):8 * (u % 2) + 8, 0:DK0],
                                       w[:, :].rearrange("p (h d) -> p h d", d=DK0), ACT.Copy), b, f"x.v{u}")

                def exps(name, scale):
                    n = b.pairs[name]
                    act.wait_ge(sc_full, b.count(PAIRS, n) + 1)
                    s.activation(PT[:, n % 2], SC[n % 2][:, :, :, :], ACT.Exp, scale=scale).then_inc(exp_done, 1)

                def query_part(m):
                    w = wait_work_full(act, b, f"{'ab'[m]}.q")
                    s.activation(parts[:, 0, 0].bitcast(F32R), w[:, :].rearrange("p (g t) -> p g t", g=2), ACT.Copy)\
                        .then_inc(qhi_ready, 1)

                def keys(m):
                    w = wait_work_full(act, b, f"{'ab'[m]}.k")
                    freed(s.activation(K1[:, :, :], w[:, :].rearrange("p (g t) -> p g t", g=2), ACT.Copy), b,
                          f"{'ab'[m]}.k")

                def key_part(m):
                    act.wait_ge(k1_ready, layer_number(b, m) + 1)
                    s.activation(parts[:, 1, 0].bitcast(F32R), K1[:, :, :], ACT.Copy).then_inc(khi_ready, 1)

                def outputs(m, p):
                    if p % 2 == 1:
                        name = f"{'ab'[m]}.Bw{p - 1}"
                        w = wait_work_full(act, b, name)
                        freed(s.activation(z_raw[:, p // 2], w[:, 0:S], ACT.Copy), b, name)

                run(b, {"x.qk": queries_keys_x, "x.v": values_x, "x.tn": lambda p: exps(f"x.tn{p}", 2.0),
                        "q": query_part, "k": keys, "first": key_part,
                        "Bt": lambda m, p: exps(f"{'ab'[m]}.Bt{p}", SCALE1), "Bw": outputs})

            body(0)
            act.wait_ge(weights1_in, 16 * len(weight_list1))
            for (_, (hi, lo)), src in zip(weight_list1, staged1):
                s.activation(hi[:, :, :].rearrange("p c n -> p (c n)"), src, ACT.Copy).then_inc(hi_ready, 1)
            with act.Fori(1, B) as i:
                body(i)
            body(B)

        @block.vector
        def _(dve):
            v = nc.vector
            for n, (_, (hi, lo)) in enumerate(weight_list):
                dve.wait_ge(hi_ready, n + 1)
                v.tensor_tensor(lo[:, :, :].rearrange("p c n -> p (c n)"), staged[n % 2],
                                hi[:, :, :].rearrange("p c n -> p (c n)").bitcast(F32), ALU.subtract)\
                    .then_inc(split_ready, 1)
            dve.wait_ge(consts_ready, 1)
            v.tensor_copy(bv_parts[0][:, :], bv_col[:, :]).then_inc(bv_step, 1)
            dve.wait_ge(bv_step, 1)
            v.tensor_tensor(bv_parts[1][:, :], bv_col[:, :], bv_parts[0][:, :].bitcast(F32), ALU.subtract)\
                .then_inc(bv_step, 1)
            dve.wait_ge(bv_step, 2)
            for k in range(2):
                for j in range(E0 // P):
                    ins = v.tensor_copy(bv_wide[k][:, j, :],
                                        bv_parts[k][:, j:j + 1].bitcast(F32).broadcast_to([P, P]))
            ins.then_inc(bv_step, 1)
            dve.wait_ge(bvo_full, 1)
            v.tensor_tensor(row["bo"], row["bo"], A[0][:, 0:D], ALU.add).then_inc(bo_ready, 1)

            def body(i):
                b = Body(i, B)

                def wait_steps():
                    dve.wait_ge(dve_step, b.total(X_STEPS, Y_STEPS, b.steps))

                def mark(ins):
                    ins.then_inc(dve_step, 1)
                    b.steps += 1

                def step(ins):
                    mark(ins)
                    wait_steps()

                def split(T, name):
                    w = wait_work_full(dve, b, name)[:, :].rearrange("p (c t) -> p c t", c=C)
                    step(v.tensor_copy(T[0][:, :, :], w))
                    return freed(v.tensor_tensor(T[1][:, :, :], w, T[0][:, :, :].bitcast(F32), ALU.subtract), b, name)

                def layer_norm(name, src, dst, gain, bias, norm_done, number):
                    for h in range(2):
                        mark(v.bn_stats(st[:, h], src[:, h]))
                    wait_steps()
                    part_wait(dve, b)
                    v.bn_aggr(mv[:, 0], st[:, 0])
                    v.bn_aggr(mv[:, 1], st[:, 1]).then_inc(stats_ready, 1)
                    n = b.count(NORMS, b.norms[name]) + 1
                    dve.wait_ge(stats_ready, n)
                    dve.wait_ge(rstd_ready, n)
                    for h in range(2):
                        mark(v.tensor_scalar(src[:, h], src[:, h], mv[:, h, 0:1], rstd[:, h:h + 1],
                                             ALU.subtract, ALU.mult))
                    wait_steps()
                    for h in range(2):
                        mark(v.tensor_tensor(src[:, h], src[:, h], row[gain], ALU.mult))
                    wait_steps()
                    for h in range(2):
                        ins = v.tensor_tensor(dst[:, h], src[:, h], row[bias], ALU.add)
                    ins.then_inc(norm_done, 1)
                    dve.wait_ge(norm_done, number)

                def transposed_inputs():
                    split(T1x, "x.xT")
                    split(T2x, "x.cT")

                def score(p):
                    slot = p % NR
                    dve.wait_ge(bias_in[slot], 16 * (NP // NR) * i + 16 * (p // NR) + 16)
                    for a in range(2):
                        dve.wait_ge(a_full[a], b.count(SCORES, b.scores[f"x.sc{p}"]) + 1)
                        part_wait(dve, b)
                        for qh in range(2):
                            s = ring[:, slot, a, qh]
                            ins = v.tensor_tensor_reduce(out=s, in0=A[a][:, qh * S:(qh + 1) * S], in1=s, scale=-1.0,
                                                         scalar=3.0e38, op0=ALU.add, op1=ALU.min,
                                                         accum_out=low[:, slot, a, qh:qh + 1])
                        ins.then_inc(a_free[a], 1)

                def divide(p):
                    w = wait_work_full(dve, b, f"x.wg{p}")[:, 0:4 * DV].rearrange("p (a h e) -> p a h e", a=2, h=2)
                    if p >= 1:
                        wait_read(dve, b, f"x.wg{p - 1}")
                    step(v.reciprocal(rec0[:, :, :], w[:, :, :, DK0]))
                    freed(v.tensor_tensor(ctx_cat[:, :, P * p:P * (p + 1)].rearrange("p h (a e) -> p a h e", a=2),
                                          w[:, :, :, 0:DK0], rec0[:, :, :].unsqueeze(3).broadcast_to([P, 2, 2, DK0]),
                                          ALU.mult), b, f"x.wg{p}")

                def norm_x():
                    dve.wait_ge(xb_ready, i + 1)
                    n = b.count(SCORES, b.scores["x.pr0"]) + 1
                    for h in range(2):
                        dve.wait_ge(a_full[h], n)
                        v.tensor_tensor(x_nat[:, h], A[h][:, 0:D], x_nat[:, h], ALU.add).then_inc(a_free[h], 1)
                    for h in range(2):
                        dve.wait_ge(a_free[h], n)
                    layer_norm("x.ln", x_nat, x1, "ln_g", "ln_b", x_norm, i + 1)

                def transposed(m):
                    src, mask = (x1, cur)[m], (mask0, mask1)[m]
                    for h in range(2):
                        step(v.tensor_scalar(junk, src[:, h], 0.0, None, ALU.not_equal, ALU.max,
                                             accum_out=mask[:, h:h + 1]))
                    if m == 1:
                        dve.wait_ge(kept, i)
                        part_wait(dve, b)
                        for h in range(2):
                            ins = v.tensor_scalar(c_keep[:, h], c_keep[:, h], mask[:, h:h + 1], 1.0, ALU.mult, ALU.mult)
                        ins.then_inc(cm_ready, 1)
                    split(T1, f"{'ab'[m]}.T")

                def query_part(m):
                    name = f"{'ab'[m]}.q"
                    w = wait_work_full(dve, b, name)[:, :].rearrange("p (g t) -> p g t", g=2)
                    dve.wait_ge(qhi_ready, layer_number(b, m) + 1)
                    v.tensor_copy(q0c[:, :], w[:, :, 0]).then_inc(q0_ready, 1)
                    freed(v.tensor_tensor(parts[:, 0, 1].bitcast(F32R), w, parts[:, 0, 0], ALU.subtract), b, name)

                def lengths(m):
                    t = "ab"[m]
                    w = wait_work_full(dve, b, f"{t}.first")
                    for gr in range(2):
                        ins = v.tensor_scalar(junk, w[:, gr * S:(gr + 1) * S], 0.0, None, ALU.not_equal,
                                              ALU.add, accum_out=length[:, gr:gr + 1])
                        if gr == 0:
                            step(ins)
                    freed(ins, b, f"{t}.first")
                    wait_read(dve, b, f"{t}.first")
                    for gr in range(2):
                        ins = v.tensor_scalar(sel_len[:, NP * gr:NP * (gr + 1)], sel[:, :], length[:, gr:gr + 1], 1.0,
                                              ALU.mult, ALU.mult)
                    ins.then_inc(sel_ready, 1)
                    wait_read(dve, b, f"{t}.k")
                    mark(v.tensor_copy(k0c[:, :], K1[:, :, 0]))
                    for gr in range(2):
                        mark(v.tensor_scalar(drop[:, gr], key_row[:, :], length[:, gr:gr + 1], None, ALU.is_ge))
                    wait_steps()
                    part_wait(dve, b)
                    v.copy_predicated(K1[:, :, :], drop, k0c[:, :].unsqueeze(2).broadcast_to([P, 2, S]))\
                        .then_inc(k1_ready, 1)

                def key_part_values(m):
                    t = "ab"[m]
                    dve.wait_ge(khi_ready, layer_number(b, m) + 1)
                    v.tensor_tensor(parts[:, 1, 1].bitcast(F32R), K1[:, :, :], parts[:, 1, 0], ALU.subtract)\
                        .then_inc(k_parts, 1)
                    w = wait_work_full(dve, b, f"{t}.len")
                    for kh in range(2):
                        ins = v.tensor_scalar(keep[:, kh], w[:, 0:H], key_col[:, kh:kh + 1], None, ALU.is_gt)
                    freed(ins, b, f"{t}.len")
                    wait_read(dve, b, f"{t}.len")
                    name = f"{t}.v"
                    w = wait_work_full(dve, b, name)
                    dve.wait_ge(q_stored, 16 * layer_number(b, m) + 16)
                    freed(v.tensor_tensor(V1[:, :, :, 0:DK1],
                                          w[:, :].rearrange("p (k h d) -> p k h d", k=2, d=DK1),
                                          keep[:, :, :].unsqueeze(3).broadcast_to([P, 2, H, DK1]), ALU.mult), b, name)
                    v.tensor_copy(V1[:, :, :, DK1:], keep[:, :, :].unsqueeze(3).broadcast_to([P, 2, H, DK1]))\
                        .then_inc(v1_ready, 1)

                def maxima(m, p):
                    for gr in range(2):
                        dve.wait_ge(a_full[gr], b.count(SCORES, b.scores[f"{'ab'[m]}.A{p}"]) + 1)
                        v.tensor_reduce(out=neg_max[:, :, NP * gr + p], in_=A[gr][:, :].rearrange(
                            "p (h t) -> p h t", h=2), axis=AX.X, op=ALU.max, negate=True).then_inc(a_free[gr], 1)

                def transposed_maxima(m):
                    w = wait_work_full(dve, b, f"{'ab'[m]}.mT")
                    freed(v.tensor_copy(max_row, w[0:H, 0:S]), b, f"{'ab'[m]}.mT")

                def norm_attention(m):
                    src, mask = (x1, cur)[m], (mask0, mask1)[m]
                    for h in range(2):
                        name = f"{'ab'[m]}.z{h}"
                        w = wait_work_full(dve, b, name)
                        zz = w[:, :].rearrange("p (u g e) -> p g u e", g=2, e=32)
                        rr = rec1[:, :].rearrange("p (g u) -> p g u", g=2)
                        step(v.reciprocal(rr, zz[:, :, :, DK1]))
                        step(v.tensor_scalar(rec1[:, :], rec1[:, :], mask[:, h:h + 1], 1.0, ALU.mult, ALU.mult))
                        freed(v.tensor_tensor(tmp[:, h].rearrange("p (g u d) -> p g u d", g=2, d=DK1),
                                              zz[:, :, :, 0:DK1],
                                              rr.unsqueeze(3).broadcast_to([P, 2, NP, DK1]), ALU.mult), b, name)
                        wait_read(dve, b, name)
                        mark(v.tensor_tensor(cur[:, h], src[:, h], tmp[:, h], ALU.add))
                    wait_steps()
                    layer_norm(f"{'ab'[m]}.z", cur, cur, ("ln1_g", "ln2_g")[m], ("ln1_b", "ln2_b")[m],
                               y_norm, 3 * i + (m - 2))

                def hidden():
                    w = wait_work_full(dve, b, "f.h")[:, :].rearrange("p (c t) -> p c t", c=C)
                    for c in range(C):
                        mark(v.tensor_scalar(tmp[:, c], w[:, c], fb_col[:, c:c + 1], 0.0, ALU.add, ALU.max))
                    wait_steps()
                    step(v.tensor_copy(T2[0][:, :, :], tmp[:, :, :]))
                    freed(v.tensor_tensor(T2[1][:, :, :], tmp[:, :, :], T2[0][:, :, :].bitcast(F32), ALU.subtract),
                          b, "f.h")

                def norm_output():
                    w = wait_work_full(dve, b, "f.o")[:, :].rearrange("p (h d) -> p h d", h=2)
                    wait_read(dve, b, "f.h")
                    for h in range(2):
                        ins = v.tensor_tensor(tmp[:, h], w[:, h], row["fc2_b"], ALU.add)
                    freed(ins, b, "f.o")
                    wait_read(dve, b, "f.o")
                    for h in range(2):
                        mark(v.scalar_tensor_tensor(cur[:, h], tmp[:, h], mask0[:, h:h + 1], cur[:, h],
                                                    ALU.mult, ALU.add))
                    wait_steps()
                    layer_norm("f.o", cur, result, "ln3_g", "ln3_b", y_norm, 3 * i)

                run(b, {"x.in": transposed_inputs, "x.sc": score, "x.wg": divide,
                        "x.ct": lambda u: split((T1x, T2x)[u % 2], f"x.ct{u}"), "x.ln": norm_x,
                        "T": transposed, "cT": lambda m: split(T2, "b.cT"), "q": query_part, "first": lengths,
                        "len": key_part_values, "A": maxima, "mT": transposed_maxima, "z": norm_attention,
                        "f.T": lambda: split(T1, "f.T"), "f.h": hidden, "f.o": norm_output})
                made = (X_STEPS if i == 0 else Y_STEPS) if b.peeled else X_STEPS + Y_STEPS
                assert b.steps == made, (b.steps, made)

            body(0)
            for n, ((_, (hi, lo)), src) in enumerate(zip(weight_list1, staged1)):
                dve.wait_ge(hi_ready, len(weight_list) + n + 1)
                v.tensor_tensor(lo[:, :, :].rearrange("p c n -> p (c n)"), src,
                                hi[:, :, :].rearrange("p c n -> p (c n)").bitcast(F32), ALU.subtract)\
                    .then_inc(split_ready, 1)
            with dve.Fori(1, B) as i:
                body(i)
            body(B)

        @block.tensor
        def _(pe):
            t = nc.tensor
            pe.wait_ge(split_ready, len(weight_list))
            pe.wait_ge(consts_ready, 1)

            def product(dst, pairs, start=True):
                terms = [(a[x], b[y]) for a, b in pairs for x, y in ((0, 0), (0, 1), (1, 0))]
                for k, (a, b) in enumerate(terms):
                    ins = t.matmul(dst, a, b, start=start and k == 0, stop=k == len(terms) - 1)
                return ins

            def cut(T, *index):
                return [part[index] for part in T]

            pe.wait_ge(bv_step, 3)
            terms = [(j, a, b) for j in range(E0 // P) for a, b in ((0, 0), (0, 1), (1, 0))]
            for k, (j, a, b) in enumerate(terms):
                ins = t.matmul(A[0][:, 0:D], bv_wide[a][:, j, :], Wo[b][:, j, :], start=k == 0, stop=k == len(terms) - 1)
            ins.then_inc(bvo_full, 1)
            pe.wait_ge(bo_ready, 1)

            every = slice(None)

            def body(i):
                b = Body(i, B)

                def transpose4(name, src):
                    w = wait_work_free(pe, b, name)
                    for c in range(C):
                        for h in range(2):
                            ins = t.transpose(w[:, c * S + h * P:c * S + (h + 1) * P], src[:, h, c * P:(c + 1) * P],
                                              ident[:, :])
                    return filled(ins, b, name)

                def transposed_inputs():
                    pe.wait_ge(x_in, 16 * i + 16)
                    transpose4("x.xT", x_nat)
                    pe.wait_ge(c_in, 16 * i + 16)
                    transpose4("x.cT", c_load)

                def values_x(u):
                    w = wait_work_free(pe, b, f"x.v{u}", ["x.cT"] if u == 0 else [])
                    kh, half = u // 2, u % 2
                    filled(product(w[:, :], [(cut(T2x, every, c, slice(kh * P, (kh + 1) * P)),
                                              cut(W0["v"], every, c, slice(512 * half, 512 * half + 512)))
                                             for c in range(C)]), b, f"x.v{u}")

                def queries_keys_x(p):
                    w = wait_work_free(pe, b, f"x.qk{p}", ["x.xT", "x.cT"] if p == 0 else [])
                    col = slice(p * P, (p + 1) * P)
                    for k, (w_, T) in enumerate(((W0["q"], T1x), (W0["k"], T2x))):
                        ins = product(w[:, k * S:(k + 1) * S],
                                      [(cut(w_, every, c, col), cut(T, every, c, every)) for c in range(C)])
                    filled(ins, b, f"x.qk{p}")

                def score(p):
                    wait_read(pe, b, f"x.qk{p}")
                    for a in range(2):
                        wait_at_least(pe, a_free[a], b.count(SCORES, b.scores[f"x.sc{p}"]))
                        for qh in range(2):
                            ins = t.matmul(A[a][:, qh * S:(qh + 1) * S], QZ0[:, a, p % 2, qh * P:(qh + 1) * P],
                                           KT0[:, p % 2, :], start=True, stop=True)
                        ins.then_inc(a_full[a], 1)

                def turn_x(p):
                    slot = b.pairs[f"x.tn{p}"] % 2
                    for a in range(2):
                        pe.wait_ge(shifted, b.total(H, 0, 2 * p + a) + 1)
                        for kh in range(2):
                            for qh in range(2):
                                ins = t.transpose(SC[slot][:, a, kh, qh * P:(qh + 1) * P],
                                                  ring[:, p % NR, a, qh, kh * P:(kh + 1) * P], ident[:, :])
                    ins.then_inc(sc_full, 1)

                def weigh_x(p):
                    n = b.pairs[f"x.tn{p}"]
                    pe.wait_ge(exp_done, b.count(PAIRS, n) + 1)
                    w = wait_work_free(pe, b, f"x.wg{p}", [f"x.v{u}" for u in range(4)] if p == 0 else [])
                    for a in range(2):
                        for qh in range(2):
                            at = (2 * a + qh) * DV
                            for kh in range(2):
                                ins = t.matmul(w[:, at:at + DV], PT[:, n % 2, a, kh, qh * P:(qh + 1) * P],
                                               V0[:, kh, 2 * p + a, :], start=kh == 0, stop=kh == 1)
                    filled(ins, b, f"x.wg{p}")

                def transposed_context(u):
                    w = wait_work_free(pe, b, f"x.ct{u}", ["x.wg6", "x.wg7"] if u == 0 else [])
                    for c in range(2):
                        for h in range(2):
                            ins = t.transpose(w[:, c * S + h * P:c * S + (h + 1) * P],
                                              ctx_cat[:, h, (2 * u + c) * P:(2 * u + c + 1) * P], ident[:, :])
                    filled(ins, b, f"x.ct{u}")

                def project(u):
                    wait_read(pe, b, f"x.ct{u}")
                    T = (T1x, T2x)[u % 2]
                    for h in range(2):
                        if u == 0:
                            wait_at_least(pe, a_free[h], b.count(SCORES, b.scores["x.pr0"]))
                        for c in range(2):
                            terms = [(T[x][:, c, h * P:(h + 1) * P], Wo[y][:, 2 * u + c, :])
                                     for x, y in ((0, 0), (0, 1), (1, 0))]
                            for k, (lhs, rhs) in enumerate(terms):
                                ins = t.matmul(A[h][:, 0:D], lhs, rhs, start=u == 0 and c == 0 and k == 0,
                                               stop=u == 3 and c == 1 and k == 2)
                        if u == 3:
                            ins.then_inc(a_full[h], 1)

                def transposed(m):
                    if m == 0:
                        pe.wait_ge(x_norm, i)
                        transpose4("a.T", x1)
                    else:
                        pe.wait_ge(y_norm, 3 * i - 2)
                        transpose4("b.T", cur)

                def transposed_masked(m):
                    pe.wait_ge(cm_ready, i)
                    transpose4("b.cT", c_keep)

                def grouped(name, weight, T, T_name):
                    w = wait_work_free(pe, b, name, [T_name])
                    for gr in range(2):
                        ins = product(w[:, gr * S:(gr + 1) * S],
                                      [(cut(weight, every, c, slice(gr * P, (gr + 1) * P)), cut(T, every, c, every))
                                       for c in range(C)])
                    filled(ins, b, name)

                def queries(m):
                    grouped(f"{'ab'[m]}.q", W1[f"q{m + 1}"], T1, f"{'ab'[m]}.T")

                def keys(m):
                    grouped(f"{'ab'[m]}.k", W1[f"k{m + 1}"], (T1, T2)[m], ("a.T", "b.cT")[m])

                def first_scores(m):
                    pe.wait_ge(q0blk_ready, layer_number(b, m) + 1)
                    w = wait_work_free(pe, b, f"{'ab'[m]}.first", [f"{'ab'[m]}.k"])
                    for gr in range(2):
                        ins = t.matmul(w[:, gr * S:(gr + 1) * S], Q0blk[:, gr], K1[:, gr], start=True, stop=True)
                    filled(ins, b, f"{'ab'[m]}.first")

                def lengths(m):
                    pe.wait_ge(sel_ready, layer_number(b, m) + 1)
                    w = wait_work_free(pe, b, f"{'ab'[m]}.len")
                    filled(t.matmul(w[:, 0:H], ones[:, :], sel_len[:, :], start=True, stop=True), b, f"{'ab'[m]}.len")

                def values(m):
                    w = wait_work_free(pe, b, f"{'ab'[m]}.v")
                    for kh in range(2):
                        ins = product(w[:, kh * D:(kh + 1) * D],
                                      [(cut((T1, T2)[m], every, c, slice(kh * P, (kh + 1) * P)),
                                        cut(W1[f"v{m + 1}"], every, c, every)) for c in range(C)])
                    filled(ins, b, f"{'ab'[m]}.v")

                def rows_of(gr, with_maximum):
                    return slice(64 * gr, 64 * gr + SPLIT + with_maximum)

                def scores(m, p):
                    if p == 0:
                        pe.wait_ge(stacks_in, 16 * STACK_LOADS * (layer_number(b, m) + 1))
                    for gr in range(2):
                        r = rows_of(gr, 0)
                        wait_at_least(pe, a_free[gr], b.count(SCORES, b.scores[f"{'ab'[m]}.A{p}"]))
                        for qh in range(2):
                            ins = t.matmul(A[gr][:, qh * S:(qh + 1) * S], QS1[r, p, qh * P:(qh + 1) * P],
                                           KS1[r, p, :], start=True, stop=m == 1)
                            if m == 0:
                                ins = t.matmul(A[gr][:, qh * S + qh * P:(qh + 1) * S], identb[:, :],
                                               mask_q[:, 0:S - qh * P], start=False, stop=True)
                        ins.then_inc(a_full[gr], 1)

                def transposed_maxima(m):
                    n = b.count(SCORES, b.scores[f"{'ab'[m]}.A{NP - 1}"]) + 1
                    for gr in range(2):
                        pe.wait_ge(a_free[gr], n)
                    w = wait_work_free(pe, b, f"{'ab'[m]}.mT")
                    for qh in range(2):
                        ins = t.transpose(w[0:H, qh * P:(qh + 1) * P], neg_max[:, qh, :], ident[:, :])
                    filled(ins, b, f"{'ab'[m]}.mT")

                def turn(m, p):
                    slot = b.pairs[f"{'ab'[m]}.Bt{p}"] % 2
                    if p == 0:
                        pe.wait_ge(max_in, 32 * (layer_number(b, m) + 1))
                    for gr in range(2):
                        r = rows_of(gr, 1)
                        for kh in range(2):
                            ins = t.matmul(SC[slot][:, gr, kh, :], KS1[r, p, kh * P:(kh + 1) * P], QS1[r, p, :],
                                           start=True, stop=m == 1)
                            if m == 0:
                                ins = t.matmul(SC[slot][:, gr, kh, 0:(kh + 1) * P], identb[:, :],
                                               mask_k[:, (1 - kh) * P:2 * P], start=False, stop=True)
                    ins.then_inc(sc_full, 1)

                def weigh(m, p):
                    n = b.pairs[f"{'ab'[m]}.Bt{p}"]
                    name = f"{'ab'[m]}.Bw{p - p % 2}"
                    if p == 0:
                        pe.wait_ge(v1_ready, layer_number(b, m) + 1)
                    pe.wait_ge(exp_done, b.count(PAIRS, n) + 1)
                    if p % 2 == 0:
                        wait_work_free(pe, b, name)
                    w = W[bank(b, name)]
                    for gr in range(2):
                        r = 32 * (2 * (p % 2) + gr)
                        for kh in range(2):
                            lo = P if m == 0 and kh == 1 else 0
                            ins = t.matmul(w[r:r + 32, lo:S], V1[:, kh, NP * gr + p, :], PT[:, n % 2, gr, kh, lo:S],
                                           start=kh == 0, stop=kh == 1, tile_position=(0, r))
                    if p % 2 == 1:
                        filled(ins, b, name)

                def outputs(m):
                    z_raws = [f"{'ab'[m]}.Bw{p}" for p in range(0, NP, 2)]
                    for h in range(2):
                        w = wait_work_free(pe, b, f"{'ab'[m]}.z{h}", z_raws if h == 0 else [])
                        for u in range(4):
                            ins = t.transpose(w[:, u * P:(u + 1) * P], z_raw[:, u, h * P:(h + 1) * P], ident[:, :])
                        filled(ins, b, f"{'ab'[m]}.z{h}")

                def transposed_stream():
                    pe.wait_ge(y_norm, 3 * i - 1)
                    transpose4("f.T", cur)

                def hidden():
                    w = wait_work_free(pe, b, "f.h", ["f.T"])
                    for c2 in range(C):
                        ins = product(w[:, c2 * S:(c2 + 1) * S],
                                      [(cut(W1["f1"], every, c, slice(c2 * P, (c2 + 1) * P)), cut(T1, every, c, every))
                                       for c in range(C)])
                    filled(ins, b, "f.h")

                def ffn_output():
                    w = wait_work_free(pe, b, "f.o", ["f.h"])
                    for h in range(2):
                        ins = product(w[:, h * D:(h + 1) * D],
                                      [(cut(T2, every, c, slice(h * P, (h + 1) * P)), cut(W1["f2"], every, c, every))
                                       for c in range(C)])
                    filled(ins, b, "f.o")

                run(b, {"x.in": transposed_inputs, "x.v": values_x, "x.qk": queries_keys_x, "x.sc": score,
                        "x.tn": turn_x, "x.wg": weigh_x, "x.ct": transposed_context, "x.pr": project,
                        "T": transposed, "cT": transposed_masked, "q": queries, "k": keys, "first": first_scores,
                        "v": values, "len": lengths, "A": scores, "mT": transposed_maxima, "Bt": turn, "Bw": weigh,
                        "z": outputs, "f.T": transposed_stream, "f.h": hidden, "f.o": ffn_output})

            body(0)
            pe.wait_ge(split_ready, len(weight_list) + len(weight_list1))
            with pe.Fori(1, B) as i:
                body(i)
            body(B)


def kernel(x, ctx_1024, fside_Bx16xSxS2_0, **v):
    import concourse.bacc as bacc
    from concourse.bass_utils import run_bass_kernel_spmd

    a0 = {k[len("L0_xattn_"):]: a for k, a in v.items() if k.startswith("L0_")}
    a1 = {k[len("L1_xattn_"):]: a for k, a in v.items() if k.startswith("L1_")}
    D = x.shape[-1]

    def heads_as_columns(w):
        return np.asarray(w).transpose(1, 0, 2).reshape(D, -1)

    arrays = {"x": x, "ctx": ctx_1024, "fside": fside_Bx16xSxS2_0}
    for n in "qkvo":
        arrays["w0" + n] = a0["w" + n]
    for n in ("q", "k", "v"):
        for layer in "12":
            arrays[f"w1{n}{layer}"] = heads_as_columns(a1[f"W{n}{layer}"])
    arrays["w1f1"] = np.asarray(a1["fc1_w"]).T
    arrays["w1f2"] = np.asarray(a1["fc2_w"]).T
    for n, a in (("bq", a0["bq"]), ("bk", a0["bk"]), ("bv", a0["bv"]), ("fb", a1["fc1_b"])):
        arrays["vec0" + n] = a
    for n, a in (("bo", a0["bo"]), ("ln_g", a0["ln_g"]), ("ln_b", a0["ln_b"]), ("fc2_b", a1["fc2_b"]),
                 ("ln1_g", a1["ln1_g"]), ("ln1_b", a1["ln1_b"]), ("ln2_g", a1["ln2_g"]), ("ln2_b", a1["ln2_b"]),
                 ("ln3_g", a1["ln3_g"]), ("ln3_b", a1["ln3_b"])):
        arrays["vec1" + n] = a
    arrays = {n: np.ascontiguousarray(a) for n, a in arrays.items()}

    nc = bacc.Bacc("TRN2", target_bir_lowering=False, num_devices=1)
    dram = {n: nc.dram_tensor("in_" + n, a.shape, mybir.dt.from_np(a.dtype), kind="ExternalInput").ap()
            for n, a in arrays.items()}

    def group(prefix):
        return {n[len(prefix):]: ap for n, ap in dram.items() if n.startswith(prefix)}

    out = nc.dram_tensor("out", x.shape, F32, kind="ExternalOutput").ap()
    build(nc, dram["x"], dram["ctx"], dram["fside"], group("w0"), group("vec0"), group("w1"), group("vec1"), out)
    r = run_bass_kernel_spmd(nc, [{"in_" + n: a for n, a in arrays.items()}], core_ids=[0])
    return r.results[0]["out"]
```
